# Optimizing a Trainium2 kernel written in Bass

```python
import numpy as np
import jax
import jax.numpy as jnp

def _softmax(x, axis=-1):
    return jax.nn.softmax(x, axis=axis)
def _gelu(x):
    return jax.nn.gelu(x, approximate=True)
def _silu(x):
    return jax.nn.silu(x)
def _sigmoid(x):
    return jax.nn.sigmoid(x)
def _layernorm(x, axis=-1, eps=1e-5):
    m = jnp.mean(x, axis=axis, keepdims=True)
    v = jnp.var(x, axis=axis, keepdims=True)
    return (x - m) / jnp.sqrt(v + eps)
def _scatter_add(tgt, idx, src, axis=0):
    return tgt.at[idx].add(src)
def _segment_sum(src, seg, n):
    return jax.ops.segment_sum(src, seg, n)

kernel_name = 'mk_adj_resnorm_d1_adj_768_01d63b'

def setup_inputs(seed: int = 0):
    np.random.seed(seed)
    _w = jnp.asarray
    def _rec_inputs():
        import jax
        import jax.numpy as jnp
        _gk = jax.random.key(seed)
        x = -0.0005963 + 1.001 * jax.random.normal(jax.random.fold_in(_gk, 1), (32, 512, 768), jnp.float32)
        _a = jax.random.bernoulli(jax.random.fold_in(_gk, 2), 0.0625, (32, 512, 512))
        adj = _a
        return x, adj
    x, adj = _rec_inputs()
    def _L0_gnn_setup():
        import jax, jax.numpy as jnp
        import numpy as np
        ATT_HEAD = 12
        IN_DIM = 768
        OUT_DIM = IN_DIM // ATT_HEAD
        LEAKY_ALPHA = 0.2
        B, N = (8, 512)
        key = jax.random.key(seed)
        ks = jax.random.split(key, 8)
        feat_in = jax.random.normal(ks[0], (B, N, IN_DIM), dtype=jnp.float32)
        adj = jax.random.randint(ks[1], (B, N, N), 0, 2) > 0
        lim_W = float(np.sqrt(6.0 / (IN_DIM + OUT_DIM)))
        W = jax.random.uniform(ks[2], (ATT_HEAD, IN_DIM, OUT_DIM), minval=-lim_W, maxval=lim_W, dtype=jnp.float32)
        b = jnp.zeros((OUT_DIM,), dtype=jnp.float32)
        lim_w = float(np.sqrt(6.0 / (OUT_DIM + 1)))
        w_src = jax.random.uniform(ks[3], (ATT_HEAD, OUT_DIM, 1), minval=-lim_w, maxval=lim_w, dtype=jnp.float32)
        w_dst = jax.random.uniform(ks[4], (ATT_HEAD, OUT_DIM, 1), minval=-lim_w, maxval=lim_w, dtype=jnp.float32)
        std_H = float(np.sqrt(2.0 / (IN_DIM + IN_DIM)))
        H_w = jax.random.normal(ks[5], (IN_DIM, IN_DIM), dtype=jnp.float32) * std_H
        H_b = jax.random.normal(ks[6], (IN_DIM,), dtype=jnp.float32) * 0.01
        return {'feat_in': feat_in, 'adj': adj, 'W': W, 'b': b, 'w_src': w_src, 'w_dst': w_dst, 'H_w': H_w, 'H_b': H_b}
    _L0_gnn_all = _L0_gnn_setup()
    _L0_gnn_in = {k: v for k, v in _L0_gnn_all.items() if k in ('W', 'b', 'w_src', 'w_dst', 'H_w', 'H_b', )}
    del _L0_gnn_all

    return {
        "x": x,
        "adj": adj,
        "L0_gnn_W": _L0_gnn_in["W"],
        "L0_gnn_b": _L0_gnn_in["b"],
        "L0_gnn_w_src": _L0_gnn_in["w_src"],
        "L0_gnn_w_dst": _L0_gnn_in["w_dst"],
        "L0_gnn_H_w": _L0_gnn_in["H_w"],
        "L0_gnn_H_b": _L0_gnn_in["H_b"],
    }

def reference(x, adj, L0_gnn_W, L0_gnn_b, L0_gnn_w_src, L0_gnn_w_dst, L0_gnn_H_w, L0_gnn_H_b):
    import jax
    import jax.numpy as jnp
    def _L0_gnn_ref(feat_in, adj, W, b, w_src, w_dst, H_w, H_b):
        import jax, jax.numpy as jnp
        import numpy as np
        ATT_HEAD = 12
        IN_DIM = 768
        OUT_DIM = IN_DIM // ATT_HEAD
        LEAKY_ALPHA = 0.2
        B, N = (8, 512)
        h = jnp.einsum('bnd,ade->bane', feat_in, W)
        th = jnp.tanh(h)
        attn_src = jnp.einsum('bane,aeo->bano', th, w_src)
        attn_dst = jnp.einsum('bane,aeo->bano', th, w_dst)
        attn = attn_src + jnp.swapaxes(attn_dst, 2, 3)
        attn = jnp.where(attn >= 0, attn, LEAKY_ALPHA * attn)
        mask = ~adj[:, None, :, :]
        attn = jnp.where(mask, jnp.float32(-999.0), attn)
        attn = jax.nn.softmax(attn, axis=-1)
        feat_out = jnp.einsum('banm,bame->bane', attn, h) + b
        feat_out = jnp.swapaxes(feat_out, 1, 2).reshape(feat_in.shape[0], feat_in.shape[1], -1)
        feat_out = jax.nn.elu(feat_out)
        gate = jax.nn.sigmoid(feat_in @ H_w.T + H_b)
        return gate * feat_out + (1.0 - gate) * feat_in

    x = _layernorm(x + _L0_gnn_ref(x, adj, L0_gnn_W, L0_gnn_b, L0_gnn_w_src, L0_gnn_w_dst, L0_gnn_H_w, L0_gnn_H_b), axis=-1)
    return x


_drawn_inputs = setup_inputs


def setup_inputs(seed=0):
    import zlib

    import numpy as np

    out = dict(_drawn_inputs(seed))
    spreads = {'L0_gnn_b': (0.0, 0.1)}
    factors = {'L0_gnn_H_b': 37.513}
    for name, (base, spread) in spreads.items():
        noise = np.random.default_rng([zlib.crc32(name.encode()), seed]).standard_normal(out[name].shape)
        drawn = base * np.exp(spread * noise) if base else spread * noise
        out[name] = jnp.asarray(drawn.astype(out[name].dtype))
    for name, factor in factors.items():
        out[name] = (out[name] * factor).astype(out[name].dtype)
    return out
```

```python
from contextlib import ExitStack

import concourse.bass as bass
from concourse import mybir

P = 128
F32 = mybir.dt.float32
F32R = mybir.dt.float32r
BF16 = mybir.dt.bfloat16
U8 = mybir.dt.uint8
ALU = mybir.AluOpType
ACT = mybir.ActivationFunctionType
AX_X = mybir.AxisListType.X



def gnn_kernel(nc, x, adj, w_all, w_src, w_dst, b, h_bias, out):
    B, N, D = x.shape
    GROUPS, COLS = w_all.shape[1], w_all.shape[2]
    HEADS, E = w_src.shape
    HG = HEADS // GROUPS
    HW = HG * E
    NT = N // P
    KC = D // P
    E2 = E + 2
    PAIR = 2 * E2
    SLOPE = 0.2
    EPS = 1e-5
    NQ = NT * HG
    assert COLS == 2 * HW and HG * PAIR <= 512 and N == 512 and GROUPS == 4 and HG == 3 and KC == 6
    UNITS = GROUPS * NT + KC + NT
    FIRST_UNITS = KC + NT + NT

    ctx = ExitStack()
    with ctx:
        def sb(name, shape, dt):
            return ctx.enter_context(nc.sbuf_tensor(name, shape, dt))

        def ps(name, shape, dt):
            return ctx.enter_context(nc.psum_tensor(name, shape, dt))

        def sem(name):
            return ctx.enter_context(nc.semaphore(name))

        w_hi = sb("w_hi", [P, KC, GROUPS, COLS], F32R)
        w_lo = sb("w_lo", [P, KC, GROUPS, COLS], F32R)
        xt_hi = sb("xt_hi", [P, KC, N], F32R)
        xt_lo = sb("xt_lo", [P, KC, N], F32R)
        xy = sb("xy", [P, 2, NT, D], F32)
        sel = sb("sel", [P, HG, NT, N], F32R)
        nadj = sb("nadj", [P, NT, N], F32R)
        hb = sb("hb", [P, NT, HG, E2], F32)
        th = sb("th", [P, NT, HW], F32)
        gate = sb("gate", [P, GROUPS, NT, HW], F32)
        wide = sb("wide", [P, NQ * PAIR], F32)
        v_hi = sb("v_hi", [P, NQ, 2, E2], F32R)
        v_lo = sb("v_lo", [P, NQ, 2, E2], F32R)
        acc = sb("acc", [P, NQ, 2, E2], F32)
        adj8 = sb("adj8", [P, 2, N], U8)
        adjb = sb("adjb", [P, 2, N], BF16)
        w_sd = sb("w_sd", [P, HEADS, 2, E], F32)
        bias1 = sb("bias1", [P, E], F32)
        d_bound = sb("d_bound", [P, HEADS], F32)
        hb3 = sb("hb3", [P, D], BF16)
        ones_b = sb("ones_b", [P, P], BF16)
        ident = sb("ident", [P, P], F32)
        ident_b = sb("ident_b", [P, P], BF16)
        minus1 = sb("minus1", [P, 1], F32)
        half = sb("half", [P, NT], F32)
        sd = sb("sd", [P, 2, NQ, 2], F32)
        sdb = sb("sdb", [P, NQ, 2], F32)
        low = sb("low", [P, NQ, 2], F32)
        ab = sb("ab", [P, 2, NQ, 2], F32)
        bb = sb("bb", [P, NQ, 2], F32)
        rden = sb("rden", [P, NQ], F32)
        stats = sb("stats", [P, NT, 2, 6], F32)
        mv = sb("mv", [P, NT, 2], F32)
        ve = sb("ve", [P, NT], F32)
        nmean = sb("nmean", [P, NT], F32)
        rstd = sb("rstd", [P, NT], F32)
        shift = sb("shift", [P, NT], F32)

        work = ps("work", [P, 2, 512], F32)
        s_row = ps("s_row", [P, 2, N], F32)
        sums = ps("sums", [P, NT, 512], F32)

        w_in = [sem("w_in0"), sem("w_in1")]
        small_in = sem("small_in")
        ones_set = sem("ones_set")
        ident_set = sem("ident_set")
        consts_set = sem("consts_set")
        gate_bias_set = sem("gate_bias_set")
        w_split_hi = sem("w_split_hi")
        w_split_lo = sem("w_split_lo")
        set_chain = sem("set_chain")
        x_in = [sem("x_in0"), sem("x_in1")]
        adj_in = [sem("adj_in0"), sem("adj_in1")]
        stored = [sem("stored0"), sem("stored1")]
        unit_full = sem("unit_full")
        s_row_full = sem("s_row_full")
        all_mask_used = sem("all_mask_used")
        head_summed = sem("head_summed")
        sums_full = sem("sums_full")
        th_done = sem("th_done")
        xt_hi_done = sem("xt_hi_done")
        adjb_done = sem("adjb_done")
        nadj_done = sem("nadj_done")
        ab_done = sem("ab_done")
        v_hi_done = sem("v_hi_done")
        exp_done = sem("exp_done")
        norm_done = sem("norm_done")
        hb_done = sem("hb_done")
        xt_lo_done = sem("xt_lo_done")
        sd_done = sem("sd_done")
        sdb_done = sem("sdb_done")
        low_done = sem("low_done")
        sel_done = sem("sel_done")
        acc_done = sem("acc_done")
        rden_done = sem("rden_done")
        elu_done = sem("elu_done")
        diff_done = sem("diff_done")
        gated_done = sem("gated_done")
        y_done = sem("y_done")
        stats_done = sem("stats_done")
        mv_done = sem("mv_done")
        ve_done = sem("ve_done")
        prod_done = sem("prod_done")
        v_done = sem("v_done")
        v_lo_done = sem("v_lo_done")
        joined_done = sem("joined_done")
        scaled_done = sem("scaled_done")
        rstd_done = sem("rstd_done")
        shift_done = sem("shift_done")

        x_v = x.rearrange("b (t p) d -> b p t d", p=P)
        out_v = out.rearrange("b (t p) d -> b p t d", p=P)
        adj_v = adj.rearrange("b p n -> (b p n)")
        w_v = w_all.rearrange("(k p) g c -> k p (g c)", p=P)

        def need(eng, s, count):
            if not isinstance(count, int) or count > 0:
                eng.wait_ge(s, count)

        def units(i, j):
            return FIRST_UNITS + UNITS * i + j + 1

        def batches(eng, body):
            body(0, 0, True)
            body(1, 1, True)
            with eng.Fori(2, B - 2, 2) as i:
                body(i, 0, True)
                body(i + 1, 1, True)
            body(B - 2, 0, True)
            body(B - 1, 1, False)

        prod_v = wide[:, 0:NQ * 2 * E].rearrange("p (q e) -> p q e", e=E)
        wide_v = wide[:, :].rearrange("p (q e) -> p q e", e=PAIR)
        hbq = hb[:, :, :, :].rearrange("p t h e -> p (t h) e")
        w_stage = [xy[:, 1, 2 * c:2 * c + 2, :].rearrange("p t d -> p (t d)") for c in range(2)]
        abs_stage = gate[:, 1, :, :].rearrange("p t c -> p (t c)")
        hb_stage = gate[:, 2, :, :].rearrange("p t c -> p (t c)")
        hb_part = gate[:, 3, :, :].rearrange("p t c -> p (t c)").bitcast(BF16)[:, 0:D]

        block = ctx.enter_context(nc.Block())

        @block.sync
        def _(sp):
            def load_adj(i, t):
                start = (NT * i + t) * P * N
                if not isinstance(i, int):
                    start = sp.snap(start)
                tile = adj_v[bass.ds(start, P * N)].rearrange("(p n) -> p n", p=P)
                need(sp, adjb_done, NT * i + t - 1)
                sp.dma_start(adj8[:, t % 2, :], tile).then_inc(adj_in[t % 2], 16)

            sp.dma_start(xy[:, 0], x_v[0]).then_inc(x_in[0], 16)
            load_adj(0, 0)
            load_adj(0, 1)
            sp.dma_start(w_sd[:, :, 0, :], w_src.partition_broadcast(P)).then_inc(small_in, 16)
            sp.dma_start(w_sd[:, :, 1, :], w_dst.partition_broadcast(P)).then_inc(small_in, 16)
            sp.dma_start(bias1[:, :], b.partition_broadcast(P)).then_inc(small_in, 16)
            sp.dma_start(hb_stage, h_bias.partition_broadcast(P)).then_inc(small_in, 16)
            for k in range(KC):
                need(sp, w_split_lo, 2 * (k - 1))
                sp.dma_start(w_stage[k % 2], w_v[k]).then_inc(w_in[k % 2], 16)
            sp.wait_ge(w_split_lo, 2 * KC)
            sp.dma_start(xy[:, 1], x_v[1]).then_inc(x_in[1], 16)
            load_adj(0, 2)
            load_adj(0, 3)

            def batch(i, par, more):
                if not (isinstance(i, int) and i == 0):
                    sp.wait_ge(norm_done, NT * i)
                    sp.dma_start(out_v[i - 1], xy[:, 1 - par]).then_inc(stored[1 - par], 16)
                    if more:
                        sp.wait_ge(stored[1 - par], 8 * (i + par))
                        sp.dma_start(xy[:, 1 - par], x_v[i + 1]).then_inc(x_in[1 - par], 16)
                if more:
                    for t in range(NT):
                        load_adj(i + 1, t)

            batches(sp, batch)
            sp.wait_ge(norm_done, NT * B)
            sp.dma_start(out_v[B - 1], xy[:, (B - 1) % 2]).then_inc(stored[(B - 1) % 2], 16)
            sp.wait_ge(stored[0], 16 * (B // 2))
            sp.wait_ge(stored[1], 16 * (B // 2))

        @block.tensor
        def _(pe):
            def release(i, j):
                j -= 2
                if j < 0:
                    i, j = i - 1, j + UNITS
                if j < 12:
                    pe.wait_ge(hb_done, 16 * i + 4 + j + 1)
                elif j < 18:
                    pe.wait_ge(xt_lo_done, KC * (i + 1) + j - 12 + 1)
                elif j < 22:
                    pe.wait_ge(hb_done, 16 * i + 16 + j - 18 + 1)
                else:
                    pe.wait_ge(nadj_done, NT * (i + 1) + j - 22 + 1)

            def transpose_x(i, k, bank):
                for t in range(NT):
                    mm = pe.transpose(work[:, bank, t * P:(t + 1) * P], xy[:, i, t, k * P:(k + 1) * P], ident[:, :])
                mm.then_inc(unit_full, 1)

            def transpose_adj(t, bank):
                dst = work[:, bank, :].bitcast(BF16)
                for m in range(NT):
                    mm = pe.transpose(dst[:, m * P:(m + 1) * P], adjb[:, t % 2, m * P:(m + 1) * P], ident_b[:, :])
                mm.then_inc(unit_full, 1)

            def project(g, m, bank):
                dst = work[:, bank, 0:COLS]
                for k in range(KC):
                    xh, xl = xt_hi[:, k, m * P:(m + 1) * P], xt_lo[:, k, m * P:(m + 1) * P]
                    pe.matmul(dst, xh, w_hi[:, k, g, :], start=(k == 0), stop=False, skip_group_check=True)
                    pe.matmul(dst, xh, w_lo[:, k, g, :], start=False, stop=False, skip_group_check=True)
                    pe.matmul(dst, xl, w_hi[:, k, g, :], start=False, stop=False, skip_group_check=True)
                pe.matmul(work[:, bank, HW:COLS], ones_b[:, :], hb3[:, g * HW:(g + 1) * HW], start=False, stop=True,
                          skip_group_check=True).then_inc(unit_full, 1)

            def spread_s(n, par, h):
                need(pe, sel_done, n - 1)
                bank = h_bank(par, h)
                for t in range(NT):
                    q = t * HG + h
                    mm = pe.transpose(s_row[:, bank, t * P:(t + 1) * P],
                                      sd[:, par, q, 0:1].to_broadcast([P, P]), ident[:, :])
                mm.then_inc(s_row_full, 1)

            def h_bank(par, h):
                return (HG * par + h) % 2

            def all_sums(i, g):
                t = GROUPS * i + g
                pe.wait_ge(v_lo_done, t + 1)
                if g == 0:
                    pe.wait_ge(nadj_done, NT * (i + 1))
                for n in range(NT):
                    need(pe, acc_done, NT * (t - 1) + n + 1)
                    dst = sums[:, n, 0:HG * PAIR].rearrange("p (h a e) -> p h a e", h=HG, a=2)[:, :, 1, :]
                    for m in range(NT):
                        for j, v in enumerate((v_hi, v_lo)):
                            mm = pe.matmul(dst, nadj[:, m, n * P:(n + 1) * P], v[:, m * HG:(m + 1) * HG, 1, :],
                                           start=(m == 0 and j == 0), stop=False, skip_group_check=True)
                mm.then_inc(all_mask_used, 1)

            def head_sums(h, n):
                dst = sums[:, n, h * PAIR:(h + 1) * PAIR]
                for m in range(NT):
                    for v in (v_hi, v_lo):
                        mm = pe.matmul(dst, sel[:, h, m, n * P:(n + 1) * P],
                                       v[:, m * HG + h, :, :].rearrange("p a e -> p (a e)"),
                                       start=False, stop=(h == HG - 1 and m == NT - 1 and v is v_lo),
                                       skip_group_check=True)
                if h == HG - 1:
                    mm.then_inc(sums_full, 1)
                elif n == NT - 1:
                    mm.then_inc(head_summed, 1)

            pe.wait_ge(ident_set, 2)
            pe.wait_ge(x_in[0], 16)
            for k in range(KC):
                need(pe, xt_lo_done, k - 1)
                transpose_x(0, k, k % 2)
            pe.wait_ge(w_split_lo, 2 * KC)
            pe.wait_ge(gate_bias_set, 1)
            pe.wait_ge(xt_lo_done, KC)
            for m in range(NT):
                need(pe, hb_done, m - 1)
                project(0, m, m % 2)
            for t in range(NT):
                if t < 2:
                    pe.wait_ge(hb_done, 3 + t)
                else:
                    pe.wait_ge(nadj_done, t - 1)
                pe.wait_ge(adjb_done, t + 1)
                transpose_adj(t, t % 2)
            pe.wait_ge(sd_done, 1)
            spread_s(0, 0, 0)
            spread_s(1, 0, 1)

            def batch(i, par, more):
                for g in range(GROUPS):
                    t = GROUPS * i + g
                    ahead = more or g < GROUPS - 1
                    first = 4 * g if g < 3 else 18
                    for m in range(NT):
                        if ahead:
                            if g == GROUPS - 1 and m == 0:
                                pe.wait_ge(xt_lo_done, KC * (i + 2))
                            release(i, first + m)
                            project((g + 1) % GROUPS, m, (first + m) % 2)
                        if m == 1:
                            spread_s(HG * t + 2, g % 2, 2)
                    all_sums(i, g)
                    for h in range(HG):
                        pe.wait_ge(sel_done, HG * t + h + 1)
                        for n in range(NT):
                            head_sums(h, n)
                            c = NT * h + n
                            if more and g == 2 and c % 2 == 1:
                                k = c // 2
                                if k == 0:
                                    pe.wait_ge(x_in[1 - par], 8 * (i + 2 + par))
                                release(i, 12 + k)
                                transpose_x(1 - par, k, k % 2)
                            if more and g == 3 and c % 3 == 2:
                                k = c // 3
                                pe.wait_ge(adjb_done, NT * (i + 1) + k + 1)
                                release(i, 22 + k)
                                transpose_adj(k, k % 2)
                    if ahead:
                        pe.wait_ge(sd_done, t + 2)
                        spread_s(HG * (t + 1), (g + 1) % 2, 0)
                        spread_s(HG * (t + 1) + 1, (g + 1) % 2, 1)

            batches(pe, batch)

        @block.scalar
        def _(act):
            def xt_high(k, count, bank):
                act.wait_ge(unit_full, count)
                nc.scalar.activation(xt_hi[:, k, :], work[:, bank, :], ACT.Copy).then_inc(xt_hi_done, 1)

            def tanhs(t, g, m, count, bank):
                act.wait_ge(unit_full, count)
                if m == 0:
                    need(act, prod_done, t)
                    need(act, y_done, t - GROUPS + 1)
                nc.scalar.activation(th[:, m, :], work[:, bank, 0:HW], ACT.Tanh)
                nc.scalar.activation(gate[:, g, m, :], work[:, bank, HW:COLS], ACT.Tanh).then_inc(th_done, 1)

            def cast_adj(i, t):
                act.wait_ge(adj_in[t % 2], 16 * (NT // 2 * i + t // 2 + 1))
                need(act, unit_full, units(i - 1, 22 + t - 2) if t >= 2 else 0)
                nc.scalar.activation(adjb[:, t % 2, :], adj8[:, t % 2, :], ACT.Copy, scale=-1.0).then_inc(adjb_done, 1)

            def mask(t, count, bank):
                act.wait_ge(unit_full, count)
                src = work[:, bank, :].bitcast(BF16)[:, 0:N].rearrange("p (m n) -> p m n", m=NT)
                nc.scalar.activation(nadj[:, :, t * P:(t + 1) * P], src, ACT.Copy).then_inc(nadj_done, 1)

            def factors(t, par):
                act.wait_ge(low_done, t + 1)
                need(act, v_done, t)
                need(act, acc_done, NT * (t - 1))
                nc.scalar.activation(ab[:, par, :, :], low[:, :, :], ACT.Exp)
                nc.scalar.activation(bb[:, :, 0], sdb[:, :, 1], ACT.Exp, scale=-1.0)
                nc.scalar.activation(bb[:, :, 1], sdb[:, :, 1], ACT.Exp, scale=-SLOPE).then_inc(ab_done, 1)

            for k in range(KC):
                xt_high(k, k + 1, k % 2)
            for k in range(KC):
                act.wait_ge(w_in[k % 2], 16 * (k // 2 + 1))
                src = w_stage[k % 2].rearrange("p (g c) -> p g c", g=GROUPS)
                nc.scalar.activation(w_hi[:, k, :, 0:HW], src[:, :, 0:HW], ACT.Copy)
                nc.scalar.activation(w_hi[:, k, :, HW:COLS], src[:, :, HW:COLS], ACT.Copy, scale=0.5)\
                    .then_inc(w_split_hi, 1)
            cast_adj(0, 0)
            cast_adj(0, 1)
            for m in range(NT):
                tanhs(0, 0, m, KC + m + 1, m % 2)
            for t in range(NT):
                mask(t, KC + NT + t + 1, t % 2)
                if t < NT - 2:
                    cast_adj(0, t + 2)
            factors(0, 0)

            def batch(i, par, more):
                for g in range(GROUPS):
                    t = GROUPS * i + g
                    ahead = more or g < GROUPS - 1
                    first = 4 * g if g < 3 else 18
                    last_step = not isinstance(i, int) or t > 0
                    act.wait_ge(v_done, t + 1)
                    need(act, sums_full, NT * t)
                    nc.scalar.activation(v_hi[:, :, :, :].rearrange("p q a e -> p (q a e)"), wide[:, :], ACT.Copy)\
                        .then_inc(v_hi_done, 1)
                    for m in range(NT):
                        if ahead:
                            tanhs(t + 1, (g + 1) % GROUPS, m, units(i, first + m), (first + m) % 2)
                        if m == 1 and last_step:
                            exp_values(t - 1)
                    if more and g == 3:
                        cast_adj(i + 1, 0)
                        cast_adj(i + 1, 1)
                        need(act, sel_done, HG * (t + 1))
                        for n in range(NT):
                            mask(n, units(i, 22 + n), n % 2)
                            if n < NT - 2:
                                cast_adj(i + 1, n + 2)
                    if more and g == 2:
                        xt_high(0, units(i, 12), 0)
                    if ahead:
                        factors(t + 1, (g + 1) % 2)
                    if more and g == 2:
                        for k in range(1, KC):
                            xt_high(k, units(i, 12 + k), k % 2)
                    if g == 0 and last_step:
                        normalise(i - 1, 1 - par)

            def exp_values(t):
                act.wait_ge(scaled_done, t + 1)
                nc.scalar.activation(acc[:, :, 1, 0:E], acc[:, :, 0, 0:E], ACT.Exp, bias=minus1[:, 0:1])\
                    .then_inc(exp_done, 1)

            def normalise(i, par):
                act.wait_ge(shift_done, i + 1)
                for n in range(NT):
                    nc.scalar.activation(xy[:, par, n, :], xy[:, par, n, :], ACT.Identity, bias=shift[:, n:n + 1],
                                         scale=rstd[:, n:n + 1]).then_inc(norm_done, 1)

            batches(act, batch)
            exp_values(GROUPS * B - 1)
            normalise(B - 1, (B - 1) % 2)

        @block.vector
        def _(dve):
            def xt_low(k, count, bank):
                dve.wait_ge(xt_hi_done, count)
                nc.vector.tensor_tensor(xt_lo[:, k, :], work[:, bank, :], xt_hi[:, k, :].bitcast(F32), ALU.subtract)\
                    .then_inc(xt_lo_done, 1)

            def values(t, m, bank):
                dve.wait_ge(th_done, NT * t + m + 1)
                need(dve, v_done, t)
                nc.vector.tensor_tensor(hb[:, m, :, 0:E], work[:, bank, 0:HW].rearrange("p (h e) -> p h e", h=HG),
                                        bias1[:, :].unsqueeze(1).to_broadcast([P, HG, E]), ALU.add)\
                    .then_inc(hb_done, 1)

            def terms(t, g, par):
                dve.wait_ge(prod_done, t + 1)
                nc.vector.tensor_reduce(sd[:, par, :, :].rearrange("p q a -> p (q a)"), prod_v, AX_X, ALU.add)\
                    .then_inc(sd_done, 1)
                dve.wait_ge(sd_done, t + 1)
                need(dve, ab_done, t)
                bound = d_bound[:, g * HG:(g + 1) * HG].unsqueeze(1).unsqueeze(3).to_broadcast([P, NT, HG, 2])
                nc.vector.tensor_tensor(sdb[:, :, :].rearrange("p (t h) a -> p t h a", t=NT),
                                        sd[:, par, :, :].rearrange("p (t h) a -> p t h a", t=NT), bound, ALU.add)\
                    .then_inc(sdb_done, 1)
                dve.wait_ge(sdb_done, t + 1)
                nc.vector.tensor_scalar(low[:, :, 0], sdb[:, :, 0], 1.0 - SLOPE, 0.0, ALU.mult, ALU.min)
                nc.vector.tensor_scalar(low[:, :, 1], sdb[:, :, 0], SLOPE - 1.0, 0.0, ALU.mult, ALU.min)\
                    .then_inc(low_done, 1)

            def select(t, par, h):
                dve.wait_ge(s_row_full, HG * t + h + 1)
                if h < HG - 1:
                    need(dve, head_summed, (HG - 1) * (t - 1) + h + 1)
                else:
                    need(dve, sums_full, NT * t)
                for m in range(NT):
                    q = m * HG + h
                    last = nc.vector.scalar_tensor_tensor(out=sel[:, h, m, :], in0=s_row[:, (HG * par + h) % 2, :],
                                                          scalar=sd[:, par, q, 1:2], in1=nadj[:, m, :].bitcast(F32),
                                                          op0=ALU.is_ge, op1=ALU.logical_and)
                last.then_inc(sel_done, 1)

            def weigh(t, par):
                for n in range(NT):
                    dve.wait_ge(sums_full, NT * t + n + 1)
                    if n == 0:
                        need(dve, y_done, t)
                    nc.vector.tensor_tensor(acc[:, n * HG:(n + 1) * HG, :, :].rearrange("p h a e -> p (h a) e"),
                                            sums[:, n, 0:HG * PAIR].rearrange("p (q e) -> p q e", e=E2),
                                            ab[:, par, n * HG:(n + 1) * HG, :].rearrange("p h a -> p (h a)")
                                            .unsqueeze(2).to_broadcast([P, 2 * HG, E2]), ALU.mult)\
                        .then_inc(acc_done, 1)

            def invert(t):
                dve.wait_ge(joined_done, t + 1)
                nc.vector.reciprocal(rden[:, :], acc[:, :, 0, E]).then_inc(rden_done, 1)

            def elu(t, g, xpar):
                f = acc[:, :, 1, 0:E]
                dve.wait_ge(exp_done, t + 1)
                nc.vector.scalar_tensor_tensor(out=f, in0=f, scalar=1.0, in1=acc[:, :, 0, 0:E],
                                               op0=ALU.min, op1=ALU.max).then_inc(elu_done, 1)
                dve.wait_ge(elu_done, t + 1)
                xg = xy[:, xpar, :, g * HW:(g + 1) * HW]
                nc.vector.scalar_tensor_tensor(out=f.rearrange("p (t h) e -> p t h e", t=NT),
                                               in0=f.rearrange("p (t h) e -> p t h e", t=NT), scalar=1.0,
                                               in1=xg.rearrange("p t (h e) -> p t h e", h=HG),
                                               op0=ALU.subtract, op1=ALU.subtract).then_inc(diff_done, 1)

            def mix(t, g, xpar):
                f = acc[:, :, 1, 0:E].rearrange("p (t h) e -> p t h e", t=NT)
                xg = xy[:, xpar, :, g * HW:(g + 1) * HW].rearrange("p t (h e) -> p t h e", h=HG)
                dve.wait_ge(diff_done, t + 1)
                nc.vector.scalar_tensor_tensor(out=f, in0=gate[:, g, :, :].rearrange("p t (h e) -> p t h e", h=HG),
                                               scalar=1.0, in1=f, op0=ALU.add, op1=ALU.mult).then_inc(gated_done, 1)
                dve.wait_ge(gated_done, t + 1)
                nc.vector.scalar_tensor_tensor(out=xg, in0=xg, scalar=4.0, in1=f, op0=ALU.mult, op1=ALU.add)\
                    .then_inc(y_done, 1)

            def moments(i, xpar):
                dve.wait_ge(y_done, GROUPS * (i + 1))
                for n in range(NT):
                    for c in range(2):
                        last = nc.vector.bn_stats(stats[:, n, c, :], xy[:, xpar, n, c * D // 2:(c + 1) * D // 2])
                last.then_inc(stats_done, 1)
                need(dve, shift_done, i)
                dve.wait_ge(stats_done, i + 1)
                nc.vector.memset(nmean[:, :], 0.0)
                for n in range(NT):
                    last = nc.vector.bn_aggr(mv[:, n, :], stats[:, n, :, :].rearrange("p c s -> p (c s)"))
                last.then_inc(mv_done, 1)
                dve.wait_ge(mv_done, i + 1)
                nc.vector.tensor_scalar(ve[:, :], mv[:, :, 1], 4.0 * EPS, None, ALU.add)
                nc.vector.tensor_scalar(nmean[:, :], mv[:, :, 0], -1.0, None, ALU.mult).then_inc(ve_done, 1)

            nc.vector.memset(hb[:, :, :, E:E + 1], 1.0)
            nc.vector.memset(hb[:, :, :, E + 1:E2], 0.0)
            nc.vector.memset(minus1[:, :], -1.0)
            nc.vector.memset(half[:, :], -0.5)
            nc.vector.memset(ones_b[:, :], 1.0)
            nc.vector.memset(hb3[:, :], 0.0).then_inc(ones_set, 1)
            for k in range(KC):
                xt_low(k, k + 1, k % 2)
            dve.wait_ge(small_in, 64)
            dve.wait_ge(ones_set, 1)

            def chained(ins, n):
                ins.then_inc(set_chain, 1)
                dve.wait_ge(set_chain, n)

            chained(nc.vector.tensor_scalar(hb_stage, hb_stage, 0.5, None, ALU.mult), 1)
            for j in range(3):
                rows = slice(32 * j, 32 * j + 1)
                chained(nc.vector.tensor_copy(hb_part, hb_stage), 3 * j + 2)
                chained(nc.vector.tensor_copy(hb3[rows, :], hb_part[rows, :]), 3 * j + 3)
                chained(nc.vector.tensor_tensor(hb_stage, hb_stage, hb_part, ALU.subtract), 3 * j + 4)
            nc.vector.tensor_scalar(bias1[:, :], bias1[:, :], 1.0, None, ALU.add)
            chained(nc.vector.scalar_tensor_tensor(out=abs_stage.rearrange("p (h e) -> p h e", h=HEADS),
                                                   in0=w_sd[:, :, 1, :], scalar=-1.0, in1=w_sd[:, :, 1, :],
                                                   op0=ALU.mult, op1=ALU.max), 11)
            nc.vector.tensor_reduce(d_bound[:, :], abs_stage.rearrange("p (h e) -> p h e", h=HEADS), AX_X, ALU.add)
            nc.vector.tensor_scalar(w_sd[:, :, 1, :], w_sd[:, :, 1, :], -1.0, None, ALU.mult)\
                .then_inc(gate_bias_set, 1)
            for k in range(KC):
                dve.wait_ge(w_split_hi, k + 1)
                src = w_stage[k % 2].rearrange("p (g c) -> p g c", g=GROUPS)
                nc.vector.tensor_tensor(w_lo[:, k, :, 0:HW], src[:, :, 0:HW], w_hi[:, k, :, 0:HW].bitcast(F32),
                                        ALU.subtract).then_inc(w_split_lo, 1)
                nc.vector.scalar_tensor_tensor(out=w_lo[:, k, :, HW:COLS], in0=src[:, :, HW:COLS], scalar=0.5,
                                               in1=w_hi[:, k, :, HW:COLS].bitcast(F32), op0=ALU.mult,
                                               op1=ALU.subtract).then_inc(w_split_lo, 1)
            for m in range(NT):
                values(0, m, m % 2)
            terms(0, 0, 0)
            dve.wait_ge(nadj_done, NT)

            def batch(i, par, more):
                for g in range(GROUPS):
                    t = GROUPS * i + g
                    ahead = more or g < GROUPS - 1
                    first = 4 * g if g < 3 else 18
                    before = not isinstance(i, int) or t > 0
                    gb, xb = (g - 1) % GROUPS, (par if g else 1 - par)
                    if before:
                        weigh(t - 1, (g + 1) % 2)
                    if g == 0:
                        dve.wait_ge(nadj_done, NT * (i + 1))
                    select(t, g % 2, 0)
                    if ahead:
                        values(t + 1, 0, first % 2)
                    if before:
                        invert(t - 1)
                    select(t, g % 2, 1)
                    if ahead:
                        values(t + 1, 1, (first + 1) % 2)
                    select(t, g % 2, 2)
                    if before:
                        elu(t - 1, gb, xb)
                    if ahead:
                        values(t + 1, 2, first % 2)
                    if before:
                        mix(t - 1, gb, xb)
                    if ahead:
                        values(t + 1, 3, (first + 1) % 2)
                    if before and g == 0:
                        moments(i - 1, 1 - par)
                    if more and g == 2:
                        xt_low(0, KC * (i + 1) + 1, 0)
                    if ahead:
                        terms(t + 1, (g + 1) % GROUPS, (g + 1) % 2)
                    if more and g == 2:
                        for k in range(1, KC):
                            xt_low(k, KC * (i + 1) + k + 1, k % 2)

            batches(dve, batch)
            last = GROUPS * B - 1
            weigh(last, 1)
            invert(last)
            elu(last, GROUPS - 1, (B - 1) % 2)
            mix(last, GROUPS - 1, (B - 1) % 2)
            moments(B - 1, (B - 1) % 2)

        @block.gpsimd
        def _(pool):
            def products(t, g):
                need(pool, v_lo_done, t)
                pool.wait_ge(th_done, NT * (t + 1))
                for a in range(2):
                    last = nc.gpsimd.tensor_tensor(
                        wide[:, 0:NQ * 2 * E].rearrange("p (q a e) -> p q a e", a=2, e=E)[:, :, a, :]
                        .rearrange("p (t h) e -> p t h e", t=NT),
                        th[:, :, :].rearrange("p t (h e) -> p t h e", h=HG),
                        w_sd[:, g * HG:(g + 1) * HG, a, :].unsqueeze(1).to_broadcast([P, NT, HG, E]), ALU.mult)
                last.then_inc(prod_done, 1)

            def scale_values(t):
                pool.wait_ge(ab_done, t + 1)
                pool.wait_ge(hb_done, NT * (t + 1))
                for a in range(2):
                    last = nc.gpsimd.tensor_tensor(wide_v[:, :, a * E2:(a + 1) * E2], hbq,
                                                   bb[:, :, a:a + 1].to_broadcast([P, NQ, E2]), ALU.mult)
                last.then_inc(v_done, 1)

            def low_part(t):
                pool.wait_ge(v_hi_done, t + 1)
                nc.gpsimd.tensor_tensor(v_lo[:, :, :, :].rearrange("p q a e -> p (q a e)"), wide[:, :],
                                        v_hi[:, :, :, :].rearrange("p q a e -> p (q a e)").bitcast(F32),
                                        ALU.subtract).then_inc(v_lo_done, 1)

            def join(t):
                pool.wait_ge(acc_done, NT * (t + 1))
                nc.gpsimd.tensor_tensor(acc[:, :, 0, :], acc[:, :, 0, :], acc[:, :, 1, :], ALU.subtract)\
                    .then_inc(joined_done, 1)

            def divide(t):
                pool.wait_ge(rden_done, t + 1)
                nc.gpsimd.tensor_tensor(acc[:, :, 0, 0:E], acc[:, :, 0, 0:E],
                                        rden[:, :].unsqueeze(2).to_broadcast([P, NQ, E]), ALU.mult)\
                    .then_inc(scaled_done, 1)

            def roots(i):
                pool.wait_ge(ve_done, i + 1)
                need(pool, norm_done, NT * i)
                nc.gpsimd.tensor_tensor(rstd[:, :], ve[:, :], half[:, :], ALU.pow).then_inc(rstd_done, 1)
                pool.wait_ge(rstd_done, i + 1)
                nc.gpsimd.tensor_tensor(shift[:, :], nmean[:, :], rstd[:, :], ALU.mult).then_inc(shift_done, 1)

            nc.gpsimd.memset(ident[:, :], 1.0).then_inc(consts_set, 1)
            pool.wait_ge(consts_set, 1)
            nc.gpsimd.affine_select(out=ident[:, :], in_=ident[:, :], compare_op=ALU.is_equal, fill=0.0, base=0,
                                    pattern=[[-1, P]], channel_multiplier=1).then_inc(ident_set, 1)
            pool.wait_ge(ident_set, 1)
            nc.gpsimd.tensor_copy(ident_b[:, :], ident[:, :]).then_inc(ident_set, 1)
            pool.wait_ge(ones_set, 1)
            pool.wait_ge(gate_bias_set, 1)
            products(0, 0)

            def batch(i, par, more):
                for g in range(GROUPS):
                    t = GROUPS * i + g
                    ahead = more or g < GROUPS - 1
                    before = not isinstance(i, int) or t > 0
                    scale_values(t)
                    if before:
                        join(t - 1)
                    low_part(t)
                    if before:
                        divide(t - 1)
                    if ahead:
                        products(t + 1, (g + 1) % GROUPS)
                    if before and g == 0:
                        roots(i - 1)

            batches(pool, batch)
            last = GROUPS * B - 1
            join(last)
            divide(last)
            roots(B - 1)


_INS = ["x", "adj", "w_all", "w_src", "w_dst", "b", "h_bias"]


def kernel(x, adj, L0_gnn_W, L0_gnn_b, L0_gnn_w_src, L0_gnn_w_dst, L0_gnn_H_w, L0_gnn_H_b):
    import numpy as _np
    import concourse.bacc as _bacc
    from concourse import mybir as _mybir
    from concourse.bass_utils import run_bass_kernel_spmd as _run

    heads, d, e = L0_gnn_W.shape
    groups = 4
    w_heads = _np.transpose(_np.asarray(L0_gnn_W), (1, 0, 2)).reshape(d, groups, -1)
    w_gate = _np.asarray(L0_gnn_H_w).T.reshape(d, groups, -1)
    laid = {
        "x": x, "adj": adj, "w_all": _np.concatenate([w_heads, w_gate], axis=2),
        "w_src": _np.asarray(L0_gnn_w_src).reshape(heads, e), "w_dst": _np.asarray(L0_gnn_w_dst).reshape(heads, e),
        "b": L0_gnn_b, "h_bias": L0_gnn_H_b,
    }
    nc = _bacc.Bacc("TRN2", target_bir_lowering=False, num_devices=1)
    arrays, args = {}, []
    for name in _INS:
        a = _np.ascontiguousarray(laid[name])
        arrays[f"in_{name}_dram"] = a
        args.append(nc.dram_tensor(f"in_{name}_dram", a.shape, _mybir.dt.from_np(a.dtype), kind="ExternalInput").ap())
    args.append(nc.dram_tensor("out_0_dram", x.shape, _mybir.dt.float32, kind="ExternalOutput").ap())
    gnn_kernel(nc, *args)
    r = _run(nc, [arrays], core_ids=[0])
    return r.results[0]["out_0_dram"]
```

```python
from contextlib import ExitStack

import concourse.bass as bass
from concourse import mybir

P = 128
F32 = mybir.dt.float32
F32R = mybir.dt.float32r
BF16 = mybir.dt.bfloat16
U8 = mybir.dt.uint8
ALU = mybir.AluOpType
ACT = mybir.ActivationFunctionType
AX_X = mybir.AxisListType.X



def gnn_kernel(nc, x, adj, w_all, w_src, w_dst, b, h_bias, out):
    B, N, D = x.shape
    GROUPS, COLS = w_all.shape[1], w_all.shape[2]
    HEADS, E = w_src.shape
    HG = HEADS // GROUPS
    HW = HG * E
    NT = N // P
    KC = D // P
    E1 = E + 1
    PAIR = 2 * E1
    QUAD = 4 * E1
    SLOPE = 0.2
    EPS = 1e-5
    NQ = NT * HG
    SUMS = NT * HG
    RING = 3
    GATES = 3
    assert COLS == 2 * HW and QUAD <= 512 and N == 512 and GROUPS == 6 and HG == 2 and KC == 6
    ADJ_STEP, X_STEP = 3, 4
    P_AT = [0, NT, 2 * NT, 3 * NT, 5 * NT, 6 * NT + KC]
    ADJ_AT, X_AT = 4 * NT, 6 * NT
    UNITS = GROUPS * NT + KC + NT
    FIRST_UNITS = KC + NT + NT

    ctx = ExitStack()
    with ctx:
        def sb(name, shape, dt):
            return ctx.enter_context(nc.sbuf_tensor(name, shape, dt))

        def ps(name, shape, dt):
            return ctx.enter_context(nc.psum_tensor(name, shape, dt))

        def sem(name):
            return ctx.enter_context(nc.semaphore(name))

        w_hi = sb("w_hi", [P, KC, GROUPS, COLS], F32R)
        w_lo = sb("w_lo", [P, KC, GROUPS, COLS], F32R)
        xt_hi = sb("xt_hi", [P, KC, N], F32R)
        xt_lo = sb("xt_lo", [P, KC, N], F32R)
        xy = sb("xy", [P, 2, NT, D], F32)
        sel = sb("sel", [P, HG, NT, N], F32R)
        nadj = sb("nadj", [P, 2, NT, N], F32R)
        hb = sb("hb", [P, NT, HG, E1], F32)
        th = sb("th", [P, NT, HW], F32)
        gate = sb("gate", [P, GATES, NT, HW], F32)
        wide = sb("wide", [P, NQ * PAIR], F32)
        v = sb("v", [P, NQ, 4, E1], F32R)
        raw = sb("raw", [P, NT, HG, 4, E1], F32)
        raw_all = sb("raw_all", [P, NT, HG, 2, E1], F32)
        b_all = sb("b_all", [P, NQ, E1], F32)
        acc = sb("acc", [P, NQ, 2, E1], F32)
        adj8 = sb("adj8", [P, NT, N], U8)
        adjb = sb("adjb", [P, 2, N], BF16)
        w_sd = sb("w_sd", [P, HEADS, 2, E], F32)
        bias1 = sb("bias1", [P, E], F32)
        d_bound = sb("d_bound", [P, HEADS], F32)
        hb3 = sb("hb3", [P, D], BF16)
        ones_b = sb("ones_b", [P, P], BF16)
        ident = sb("ident", [P, P], F32)
        ident_b = sb("ident_b", [P, P], BF16)
        minus1 = sb("minus1", [P, 1], F32)
        half = sb("half", [P, NT], F32)
        sd = sb("sd", [P, 2, NQ, 2], F32)
        sdb = sb("sdb", [P, NQ, 2], F32)
        log_rho = sb("log_rho", [P, NQ], F32)
        rho = sb("rho", [P, 2, NQ], F32)
        bb = sb("bb", [P, NQ, 2], F32)
        rden = sb("rden", [P, NQ], F32)
        stats = sb("stats", [P, NT, GROUPS, 6], F32)
        mv = sb("mv", [P, NT, 2], F32)
        ve = sb("ve", [P, NT], F32)
        nmean = sb("nmean", [P, NT], F32)
        rstd = sb("rstd", [P, NT], F32)
        shift = sb("shift", [P, NT], F32)

        work = ps("work", [P, 2, 512], F32)
        s_row = ps("s_row", [P, 2, N], F32)
        head_sum = ps("head_sum", [P, RING, 512], F32)
        all_sum = ps("all_sum", [P, 1, 512], F32)

        w_in = [sem("w_in0"), sem("w_in1")]
        small_in = sem("small_in")
        ones_set = sem("ones_set")
        ident_set = sem("ident_set")
        consts_set = sem("consts_set")
        gate_bias_set = sem("gate_bias_set")
        w_split_hi = sem("w_split_hi")
        w_split_lo = sem("w_split_lo")
        set_chain = sem("set_chain")
        x_in = [sem("x_in0"), sem("x_in1")]
        adj_in = sem("adj_in")
        stored = [sem("stored0"), sem("stored1")]
        unit_full = sem("unit_full")
        s_row_full = sem("s_row_full")
        all_sum_full = sem("all_sum_full")
        head_sum_full = sem("head_sum_full")
        th_done = sem("th_done")
        xt_hi_done = sem("xt_hi_done")
        adjb_done = sem("adjb_done")
        nadj_done = sem("nadj_done")
        factors_done = sem("factors_done")
        v_hi_done = sem("v_hi_done")
        exp_done = sem("exp_done")
        raw_done = sem("raw_done")
        raw_all_done = sem("raw_all_done")
        norm_done = sem("norm_done")
        hb_done = sem("hb_done")
        xt_lo_done = sem("xt_lo_done")
        sd_done = sem("sd_done")
        sdb_done = sem("sdb_done")
        log_rho_done = sem("log_rho_done")
        sel_done = sem("sel_done")
        whole_done = sem("whole_done")
        acc_done = sem("acc_done")
        rden_done = sem("rden_done")
        elu_done = sem("elu_done")
        diff_done = sem("diff_done")
        gated_done = sem("gated_done")
        y_done = sem("y_done")
        stats_done = sem("stats_done")
        mv_done = sem("mv_done")
        ve_done = sem("ve_done")
        prod_done = sem("prod_done")
        v_done = sem("v_done")
        v_lo_done = sem("v_lo_done")
        b_all_done = sem("b_all_done")
        rest_done = sem("rest_done")
        joined_done = sem("joined_done")
        scaled_done = sem("scaled_done")
        rstd_done = sem("rstd_done")
        shift_done = sem("shift_done")

        x_v = x.rearrange("b (t p) d -> b p t d", p=P)
        out_v = out.rearrange("b (t p) d -> b p t d", p=P)
        adj_v = adj.rearrange("b p n -> (b p n)")
        w_v = w_all.rearrange("(k p) g c -> k p (g c)", p=P)

        def need(eng, s, count):
            if not isinstance(count, int) or count > 0:
                eng.wait_ge(s, count)

        def units(i, j):
            return FIRST_UNITS + UNITS * i + j + 1

        def first_unit(g, more):
            return P_AT[g] if more or g < ADJ_STEP + 1 else ADJ_AT

        def batches(eng, body):
            body(0, 0, True)
            body(1, 1, True)
            with eng.Fori(2, B - 2, 2) as i:
                body(i, 0, True)
                body(i + 1, 1, True)
            body(B - 2, 0, True)
            body(B - 1, 1, False)

        prod_v = wide[:, 0:NQ * 2 * E].rearrange("p (q e) -> p q e", e=E)
        wide_v = wide[:, :].rearrange("p (q e) -> p q e", e=PAIR)
        hbq = hb[:, :, :, :].rearrange("p t h e -> p (t h) e")
        v_parts = v[:, :, :, :].rearrange("p q (a s) e -> p (q a) s e", s=2)
        wide_parts = wide[:, :].rearrange("p (q e) -> p q e", e=E1)
        w_stage = [xy[:, 1, 2 * c:2 * c + 2, :].rearrange("p t d -> p (t d)") for c in range(2)]
        raw_flat = raw[:, :, :, :, :].rearrange("p t h s e -> p (t h s e)")
        abs_stage = raw_flat[:, 0:D]
        hb_stage = raw_flat[:, D:2 * D]
        hb_part = acc[:, :, :, :].rearrange("p q a e -> p (q a e)").bitcast(BF16)[:, 0:D]

        block = ctx.enter_context(nc.Block())

        @block.sync
        def _(sp):
            def load_adj(i):
                start = NT * i * P * N
                if not isinstance(i, int):
                    start = sp.snap(start)
                rows = adj_v[bass.ds(start, N * N)].rearrange("(t p n) -> p t n", p=P, n=N)
                need(sp, adjb_done, NT * i)
                sp.dma_start(adj8[:, :, :], rows).then_inc(adj_in, 16)

            sp.dma_start(xy[:, 0], x_v[0]).then_inc(x_in[0], 16)
            load_adj(0)
            sp.dma_start(w_sd[:, :, 0, :], w_src.partition_broadcast(P)).then_inc(small_in, 16)
            sp.dma_start(w_sd[:, :, 1, :], w_dst.partition_broadcast(P)).then_inc(small_in, 16)
            sp.dma_start(bias1[:, :], b.partition_broadcast(P)).then_inc(small_in, 16)
            sp.dma_start(hb_stage, h_bias.partition_broadcast(P)).then_inc(small_in, 16)
            for k in range(KC):
                need(sp, w_split_lo, 2 * (k - 1))
                sp.dma_start(w_stage[k % 2], w_v[k]).then_inc(w_in[k % 2], 16)
            sp.wait_ge(w_split_lo, 2 * KC)
            sp.dma_start(xy[:, 1], x_v[1]).then_inc(x_in[1], 16)

            def batch(i, par, more):
                if more:
                    load_adj(i + 1)
                if not (isinstance(i, int) and i == 0):
                    sp.wait_ge(norm_done, NT * i)
                    sp.dma_start(out_v[i - 1], xy[:, 1 - par]).then_inc(stored[1 - par], 16)
                    if more:
                        sp.wait_ge(stored[1 - par], 8 * (i + par))
                        sp.dma_start(xy[:, 1 - par], x_v[i + 1]).then_inc(x_in[1 - par], 16)

            batches(sp, batch)
            sp.wait_ge(norm_done, NT * B)
            sp.dma_start(out_v[B - 1], xy[:, (B - 1) % 2]).then_inc(stored[(B - 1) % 2], 16)
            sp.wait_ge(stored[0], 16 * (B // 2))
            sp.wait_ge(stored[1], 16 * (B // 2))

        @block.tensor
        def _(pe):
            def release(i, j, more):
                j -= 2
                if j < 0:
                    i, j, more = i - 1, j + UNITS, True
                if j < ADJ_AT or not more:
                    pe.wait_ge(hb_done, GROUPS * NT * i + NT + j + 1)
                elif j < P_AT[4]:
                    pe.wait_ge(nadj_done, NT * (i + 1) + j - ADJ_AT + 1)
                elif j < X_AT:
                    pe.wait_ge(hb_done, GROUPS * NT * i + NT + j - NT + 1)
                elif j < P_AT[5]:
                    pe.wait_ge(xt_lo_done, KC * (i + 1) + j - X_AT + 1)
                else:
                    pe.wait_ge(hb_done, GROUPS * NT * (i + 1) + j - P_AT[5] + 1)

            def transpose_x(i, k, bank):
                for t in range(NT):
                    mm = pe.transpose(work[:, bank, t * P:(t + 1) * P], xy[:, i, t, k * P:(k + 1) * P], ident[:, :])
                mm.then_inc(unit_full, 1)

            def transpose_adj(t, bank):
                dst = work[:, bank, :].bitcast(BF16)
                for m in range(NT):
                    mm = pe.transpose(dst[:, m * P:(m + 1) * P], adjb[:, t % 2, m * P:(m + 1) * P], ident_b[:, :])
                mm.then_inc(unit_full, 1)

            def project(g, m, bank):
                dst = work[:, bank, 0:COLS]
                for k in range(KC):
                    xh, xl = xt_hi[:, k, m * P:(m + 1) * P], xt_lo[:, k, m * P:(m + 1) * P]
                    pe.matmul(dst, xh, w_hi[:, k, g, :], start=(k == 0), stop=False, skip_group_check=True)
                    pe.matmul(dst, xh, w_lo[:, k, g, :], start=False, stop=False, skip_group_check=True)
                    pe.matmul(dst, xl, w_hi[:, k, g, :], start=False, stop=False, skip_group_check=True)
                pe.matmul(work[:, bank, HW:COLS], ones_b[:, :], hb3[:, g * HW:(g + 1) * HW], start=False, stop=True,
                          skip_group_check=True).then_inc(unit_full, 1)

            def spread_s(t, par, h):
                need(pe, sel_done, HG * (t - 1) + h + 1)
                for m in range(NT):
                    mm = pe.transpose(s_row[:, h, m * P:(m + 1) * P],
                                      sd[:, par, m * HG + h, 0:1].to_broadcast([P, P]), ident[:, :])
                mm.then_inc(s_row_full, 1)

            def sum_all(i, t, par, n):
                need(pe, raw_all_done, NT * t + n)
                for m in range(NT):
                    mm = pe.matmul(all_sum[:, 0, 0:QUAD], nadj[:, par, m, n * P:(n + 1) * P],
                                   v[:, m * HG:(m + 1) * HG, 2:4, :].rearrange("p h s e -> p h (s e)"),
                                   start=(m == 0), stop=(m == NT - 1))
                mm.then_inc(all_sum_full, 1)

            def sum_head(t, g, h, n):
                c = NT * h + n
                need(pe, raw_done, SUMS * t + c - RING + 1)
                for m in range(NT):
                    mm = pe.matmul(head_sum[:, (SUMS * g + c) % RING, 0:QUAD], sel[:, h, m, n * P:(n + 1) * P],
                                   v[:, m * HG + h, :, :].rearrange("p s e -> p (s e)"),
                                   start=(m == 0), stop=(m == NT - 1))
                mm.then_inc(head_sum_full, 1)

            pe.wait_ge(ident_set, 2)
            pe.wait_ge(x_in[0], 16)
            for k in range(KC):
                need(pe, xt_lo_done, k - 1)
                transpose_x(0, k, k % 2)
            for t in range(NT):
                if t < 2:
                    pe.wait_ge(xt_lo_done, KC - 1 + t)
                else:
                    pe.wait_ge(nadj_done, t - 1)
                pe.wait_ge(adjb_done, t + 1)
                transpose_adj(t, t % 2)
            pe.wait_ge(w_split_lo, 2 * KC)
            pe.wait_ge(gate_bias_set, 1)
            for m in range(NT):
                if m < 2:
                    pe.wait_ge(nadj_done, NT - 1 + m)
                else:
                    pe.wait_ge(hb_done, m - 1)
                project(0, m, m % 2)
            pe.wait_ge(sd_done, 1)
            for h in range(HG):
                spread_s(0, 0, h)

            def batch(i, par, more):
                for g in range(GROUPS):
                    t = GROUPS * i + g
                    ahead = more or g < GROUPS - 1

                    def project_ahead(m):
                        if ahead:
                            if g == GROUPS - 1 and m == 0:
                                pe.wait_ge(xt_lo_done, KC * (i + 2))
                            release(i, first_unit(g, more) + m, more)
                            project((g + 1) % GROUPS, m, m % 2)

                    for m in range(NT):
                        project_ahead(m)
                    pe.wait_ge(v_lo_done, t + 1)
                    if g == 0:
                        pe.wait_ge(nadj_done, NT * (i + 1))
                    for h in range(HG):
                        for n in range(NT):
                            c = NT * h + n
                            if c % 2 == 0:
                                sum_all(i, t, par, c // 2)
                            if n == 0:
                                pe.wait_ge(sel_done, HG * t + h + 1)
                            sum_head(t, g, h, n)
                            if more and g == ADJ_STEP and c % 2 == 1:
                                k = c // 2
                                pe.wait_ge(adjb_done, NT * (i + 1) + k + 1)
                                release(i, ADJ_AT + k, more)
                                transpose_adj(k, k % 2)
                            if more and g == X_STEP and 1 <= c <= KC:
                                k = c - 1
                                if k == 0:
                                    pe.wait_ge(x_in[1 - par], 8 * (i + 2 + par))
                                release(i, X_AT + k, more)
                                transpose_x(1 - par, k, k % 2)
                    if ahead:
                        pe.wait_ge(sd_done, t + 2)
                        for h in range(HG):
                            spread_s(t + 1, (g + 1) % 2, h)

            batches(pe, batch)

        @block.scalar
        def _(act):
            def xt_high(k, count, bank):
                act.wait_ge(unit_full, count)
                nc.scalar.activation(xt_hi[:, k, :], work[:, bank, :], ACT.Copy).then_inc(xt_hi_done, 1)

            def tanhs(t, g, m, count, bank):
                act.wait_ge(unit_full, count)
                if m == 0:
                    need(act, prod_done, 2 * t)
                    need(act, y_done, t - GATES + 1)
                nc.scalar.activation(th[:, m, :], work[:, bank, 0:HW], ACT.Tanh)
                nc.scalar.activation(gate[:, g % GATES, m, :], work[:, bank, HW:COLS], ACT.Tanh).then_inc(th_done, 1)

            def cast_adj(i, t):
                act.wait_ge(adj_in, 16 * (i + 1))
                need(act, unit_full, units(i - 1, ADJ_AT + t - 2) if t >= 2 else 0)
                nc.scalar.activation(adjb[:, t % 2, :], adj8[:, t, :], ACT.Copy, scale=-1.0).then_inc(adjb_done, 1)

            def mask(t, par, count, bank):
                act.wait_ge(unit_full, count)
                src = work[:, bank, :].bitcast(BF16)[:, 0:N].rearrange("p (m n) -> p m n", m=NT)
                nc.scalar.activation(nadj[:, par, :, t * P:(t + 1) * P], src, ACT.Copy).then_inc(nadj_done, 1)

            def factors(t, par):
                act.wait_ge(log_rho_done, t + 1)
                need(act, v_done, t)
                need(act, acc_done, t - 1)
                nc.scalar.activation(rho[:, par, :], log_rho[:, :], ACT.Exp)
                nc.scalar.activation(bb[:, :, 0], sdb[:, :, 1], ACT.Exp, scale=-1.0)
                nc.scalar.activation(bb[:, :, 1], sdb[:, :, 1], ACT.Exp, scale=-SLOPE).then_inc(factors_done, 1)

            for k in range(KC):
                xt_high(k, k + 1, k % 2)
            cast_adj(0, 0)
            cast_adj(0, 1)
            for t in range(NT):
                mask(t, 0, KC + t + 1, t % 2)
                if t < NT - 2:
                    cast_adj(0, t + 2)
            for k in range(KC):
                act.wait_ge(w_in[k % 2], 16 * (k // 2 + 1))
                src = w_stage[k % 2].rearrange("p (g c) -> p g c", g=GROUPS)
                nc.scalar.activation(w_hi[:, k, :, 0:HW], src[:, :, 0:HW], ACT.Copy)
                nc.scalar.activation(w_hi[:, k, :, HW:COLS], src[:, :, HW:COLS], ACT.Copy, scale=0.5)\
                    .then_inc(w_split_hi, 1)
            for m in range(NT):
                tanhs(0, 0, m, KC + NT + m + 1, m % 2)
            factors(0, 0)

            def v_high(t):
                act.wait_ge(v_done, t + 1)
                need(act, head_sum_full, SUMS * t)
                nc.scalar.activation(v_parts[:, :, 0, :], wide_parts, ACT.Copy).then_inc(v_hi_done, 1)

            def read_all(t, n):
                act.wait_ge(all_sum_full, NT * t + n + 1)
                if n == 0:
                    need(act, b_all_done, t)
                nc.scalar.activation(raw_all[:, n, :, :, :].rearrange("p h s e -> p (h s e)"),
                                     all_sum[:, 0, 0:QUAD], ACT.Copy).then_inc(raw_all_done, 1)

            def read_head(t, g, c):
                h, n = c // NT, c % NT
                act.wait_ge(head_sum_full, SUMS * t + c + 1)
                if n == 0:
                    need(act, whole_done, HG * (t - 1) + h + 1)
                nc.scalar.activation(raw[:, n, h, :, :].rearrange("p s e -> p (s e)"),
                                     head_sum[:, (SUMS * g + c) % RING, 0:QUAD], ACT.Copy).then_inc(raw_done, 1)

            def batch(i, par, more):
                for g in range(GROUPS):
                    t = GROUPS * i + g
                    ahead = more or g < GROUPS - 1
                    before = not isinstance(i, int) or t > 0
                    v_high(t)
                    if more and g == ADJ_STEP:
                        cast_adj(i + 1, 0)
                        cast_adj(i + 1, 1)
                    for m in range(NT):
                        if ahead:
                            tanhs(t + 1, (g + 1) % GROUPS, m, units(i, first_unit(g, more) + m), m % 2)
                        if g == 1 and not (isinstance(i, int) and i == 0):
                            normalise(i - 1, 1 - par, m)
                    for c in range(SUMS):
                        if c % 2 == 0:
                            read_all(t, c // 2)
                        read_head(t, g, c)
                        if c == 0 and before:
                            exp_values(t - 1)
                        if c == 4 and ahead:
                            factors(t + 1, (g + 1) % 2)
                        if more and g == ADJ_STEP and c % 2 == 1:
                            n = c // 2
                            mask(n, 1 - par, units(i, ADJ_AT + n), n % 2)
                            if n < NT - 2:
                                cast_adj(i + 1, n + 2)
                        if more and g == X_STEP and 1 <= c <= KC:
                            xt_high(c - 1, units(i, X_AT + c - 1), (c - 1) % 2)

            def exp_values(t):
                act.wait_ge(scaled_done, t + 1)
                nc.scalar.activation(acc[:, :, 1, 0:E], acc[:, :, 0, 0:E], ACT.Exp, bias=minus1[:, 0:1])\
                    .then_inc(exp_done, 1)

            def normalise(i, par, n):
                act.wait_ge(shift_done, i + 1)
                nc.scalar.activation(xy[:, par, n, :], xy[:, par, n, :], ACT.Identity, bias=shift[:, n:n + 1],
                                     scale=rstd[:, n:n + 1]).then_inc(norm_done, 1)

            batches(act, batch)
            exp_values(GROUPS * B - 1)
            for n in range(NT):
                normalise(B - 1, (B - 1) % 2, n)

        @block.vector
        def _(dve):
            def xt_low(k, count, bank):
                dve.wait_ge(xt_hi_done, count)
                nc.vector.tensor_tensor(xt_lo[:, k, :], work[:, bank, :], xt_hi[:, k, :].bitcast(F32), ALU.subtract)\
                    .then_inc(xt_lo_done, 1)

            def values(t, m, bank):
                dve.wait_ge(th_done, NT * t + m + 1)
                need(dve, v_done, t)
                nc.vector.tensor_tensor(hb[:, m, :, 0:E], work[:, bank, 0:HW].rearrange("p (h e) -> p h e", h=HG),
                                        bias1[:, :].unsqueeze(1).to_broadcast([P, HG, E]), ALU.add)\
                    .then_inc(hb_done, 1)

            def terms(t, g, par):
                dve.wait_ge(prod_done, 2 * (t + 1))
                nc.vector.tensor_reduce(sd[:, par, :, :].rearrange("p q a -> p (q a)"), prod_v, AX_X, ALU.add)\
                    .then_inc(sd_done, 1)
                dve.wait_ge(sd_done, t + 1)
                need(dve, factors_done, t)
                bound = d_bound[:, g * HG:(g + 1) * HG].unsqueeze(1).unsqueeze(3).to_broadcast([P, NT, HG, 2])
                nc.vector.tensor_tensor(sdb[:, :, :].rearrange("p (t h) a -> p t h a", t=NT),
                                        sd[:, par, :, :].rearrange("p (t h) a -> p t h a", t=NT), bound, ALU.add)\
                    .then_inc(sdb_done, 1)
                dve.wait_ge(sdb_done, t + 1)
                nc.vector.tensor_scalar(log_rho[:, :], sdb[:, :, 0], SLOPE - 1.0, 0.0, ALU.mult, ALU.min)\
                    .then_inc(log_rho_done, 1)

            def select(t, par, mpar, h, tiles):
                if tiles[0] == 0:
                    dve.wait_ge(s_row_full, HG * t + h + 1)
                    need(dve, head_sum_full, SUMS * (t - 1) + NT * (h + 1))
                for m in tiles:
                    last = nc.vector.scalar_tensor_tensor(out=sel[:, h, m, :], in0=s_row[:, h, :],
                                                          scalar=sd[:, par, m * HG + h, 1:2],
                                                          in1=nadj[:, mpar, m, :].bitcast(F32),
                                                          op0=ALU.is_ge, op1=ALU.logical_and)
                if tiles[-1] == NT - 1:
                    last.then_inc(sel_done, 1)

            def whole(t, h):
                dve.wait_ge(raw_done, SUMS * t + NT * (h + 1))
                need(dve, y_done, t)
                parts = raw[:, :, h, :, :].rearrange("p t (a s) e -> p t a s e", s=2)
                nc.vector.tensor_tensor(acc[:, :, :, :].rearrange("p (t h) a e -> p t h a e", t=NT)[:, :, h, :, :],
                                        parts[:, :, :, 0, :], parts[:, :, :, 1, :], ALU.add).then_inc(whole_done, 1)

            def weigh(t, par):
                dve.wait_ge(rest_done, t + 1)
                nc.vector.tensor_tensor(acc[:, :, 1, :], acc[:, :, 1, :],
                                        rho[:, par, :].unsqueeze(2).to_broadcast([P, NQ, E1]), ALU.mult)\
                    .then_inc(acc_done, 1)

            def invert(t):
                dve.wait_ge(joined_done, t + 1)
                nc.vector.reciprocal(rden[:, :], acc[:, :, 0, E]).then_inc(rden_done, 1)

            def elu(t, g, xpar):
                f = acc[:, :, 1, 0:E]
                dve.wait_ge(exp_done, t + 1)
                nc.vector.scalar_tensor_tensor(out=f, in0=f, scalar=1.0, in1=acc[:, :, 0, 0:E],
                                               op0=ALU.min, op1=ALU.max).then_inc(elu_done, 1)
                dve.wait_ge(elu_done, t + 1)
                xg = xy[:, xpar, :, g * HW:(g + 1) * HW]
                nc.vector.scalar_tensor_tensor(out=f.rearrange("p (t h) e -> p t h e", t=NT),
                                               in0=f.rearrange("p (t h) e -> p t h e", t=NT), scalar=1.0,
                                               in1=xg.rearrange("p t (h e) -> p t h e", h=HG),
                                               op0=ALU.subtract, op1=ALU.subtract).then_inc(diff_done, 1)

            def mix(t, g, xpar):
                f = acc[:, :, 1, 0:E].rearrange("p (t h) e -> p t h e", t=NT)
                xg = xy[:, xpar, :, g * HW:(g + 1) * HW].rearrange("p t (h e) -> p t h e", h=HG)
                dve.wait_ge(diff_done, t + 1)
                nc.vector.scalar_tensor_tensor(out=f, in0=gate[:, g % GATES, :, :].rearrange("p t (h e) -> p t h e", h=HG),
                                               scalar=1.0, in1=f, op0=ALU.add, op1=ALU.mult).then_inc(gated_done, 1)
                dve.wait_ge(gated_done, t + 1)
                nc.vector.scalar_tensor_tensor(out=xg, in0=xg, scalar=4.0, in1=f, op0=ALU.mult, op1=ALU.add)\
                    .then_inc(y_done, 1)

            def moments(t, g, xpar):
                dve.wait_ge(y_done, t + 1)
                for n in range(NT):
                    last = nc.vector.bn_stats(stats[:, n, g, :], xy[:, xpar, n, g * HW:(g + 1) * HW])
                if g == GROUPS - 1:
                    last.then_inc(stats_done, 1)

            def row_moments(i):
                need(dve, shift_done, i)
                dve.wait_ge(stats_done, i + 1)
                nc.vector.memset(nmean[:, :], 0.0)
                for n in range(NT):
                    last = nc.vector.bn_aggr(mv[:, n, :], stats[:, n, :, :].rearrange("p c s -> p (c s)"))
                last.then_inc(mv_done, 1)
                dve.wait_ge(mv_done, i + 1)
                nc.vector.tensor_scalar(ve[:, :], mv[:, :, 1], 4.0 * EPS, None, ALU.add)
                nc.vector.tensor_scalar(nmean[:, :], mv[:, :, 0], -1.0, None, ALU.mult).then_inc(ve_done, 1)

            nc.vector.memset(hb[:, :, :, E:E + 1], 1.0)
            nc.vector.memset(minus1[:, :], -1.0)
            nc.vector.memset(half[:, :], -0.5)
            nc.vector.memset(ones_b[:, :], 1.0)
            nc.vector.memset(hb3[:, :], 0.0).then_inc(ones_set, 1)
            for k in range(KC):
                xt_low(k, k + 1, k % 2)
            dve.wait_ge(small_in, 64)
            dve.wait_ge(ones_set, 1)

            def chained(ins, n):
                ins.then_inc(set_chain, 1)
                dve.wait_ge(set_chain, n)

            chained(nc.vector.tensor_scalar(hb_stage, hb_stage, 0.5, None, ALU.mult), 1)
            for j in range(3):
                rows = slice(32 * j, 32 * j + 1)
                chained(nc.vector.tensor_copy(hb_part, hb_stage), 3 * j + 2)
                chained(nc.vector.tensor_copy(hb3[rows, :], hb_part[rows, :]), 3 * j + 3)
                chained(nc.vector.tensor_tensor(hb_stage, hb_stage, hb_part, ALU.subtract), 3 * j + 4)
            nc.vector.tensor_scalar(bias1[:, :], bias1[:, :], 1.0, None, ALU.add)
            chained(nc.vector.scalar_tensor_tensor(out=abs_stage.rearrange("p (h e) -> p h e", h=HEADS),
                                                   in0=w_sd[:, :, 1, :], scalar=-1.0, in1=w_sd[:, :, 1, :],
                                                   op0=ALU.mult, op1=ALU.max), 11)
            nc.vector.tensor_reduce(d_bound[:, :], abs_stage.rearrange("p (h e) -> p h e", h=HEADS), AX_X, ALU.add)
            nc.vector.tensor_scalar(w_sd[:, :, 1, :], w_sd[:, :, 1, :], -1.0, None, ALU.mult)\
                .then_inc(gate_bias_set, 1)
            for k in range(KC):
                dve.wait_ge(w_split_hi, k + 1)
                src = w_stage[k % 2].rearrange("p (g c) -> p g c", g=GROUPS)
                nc.vector.tensor_tensor(w_lo[:, k, :, 0:HW], src[:, :, 0:HW], w_hi[:, k, :, 0:HW].bitcast(F32),
                                        ALU.subtract).then_inc(w_split_lo, 1)
                nc.vector.scalar_tensor_tensor(out=w_lo[:, k, :, HW:COLS], in0=src[:, :, HW:COLS], scalar=0.5,
                                               in1=w_hi[:, k, :, HW:COLS].bitcast(F32), op0=ALU.mult,
                                               op1=ALU.subtract).then_inc(w_split_lo, 1)
            for m in range(NT):
                values(0, m, m % 2)
            terms(0, 0, 0)

            def batch(i, par, more):
                later = not (isinstance(i, int) and i == 0)
                for g in range(GROUPS):
                    t = GROUPS * i + g
                    ahead = more or g < GROUPS - 1
                    before = later or g > 0
                    gb, xb = (g - 1) % GROUPS, (par if g else 1 - par)
                    if g == 0:
                        dve.wait_ge(nadj_done, NT * (i + 1))
                    select(t, g % 2, par, 0, [0, 1, 2, 3])
                    if ahead:
                        values(t + 1, 0, 0)
                    if before:
                        whole(t - 1, 0)
                        whole(t - 1, 1)
                    select(t, g % 2, par, 1, [0, 1])
                    if ahead:
                        values(t + 1, 1, 1)
                    if before:
                        weigh(t - 1, (g + 1) % 2)
                    select(t, g % 2, par, 1, [2, 3])
                    if before:
                        invert(t - 1)
                    if ahead:
                        values(t + 1, 2, 0)
                        values(t + 1, 3, 1)
                    if before:
                        elu(t - 1, gb, xb)
                    if more and g == X_STEP:
                        for k in range(2):
                            xt_low(k, KC * (i + 1) + k + 1, k % 2)
                    if ahead:
                        terms(t + 1, (g + 1) % GROUPS, (g + 1) % 2)
                    if before:
                        mix(t - 1, gb, xb)
                        moments(t - 1, gb, xb)
                    if later and g == 0:
                        row_moments(i - 1)
                    if more and g == X_STEP:
                        for k in range(2, KC):
                            xt_low(k, KC * (i + 1) + k + 1, k % 2)

            batches(dve, batch)
            last = GROUPS * B - 1
            for h in range(HG):
                whole(last, h)
            weigh(last, 1)
            invert(last)
            elu(last, GROUPS - 1, (B - 1) % 2)
            mix(last, GROUPS - 1, (B - 1) % 2)
            moments(last, GROUPS - 1, (B - 1) % 2)
            row_moments(B - 1)

        @block.gpsimd
        def _(pool):
            def products(t, g, half):
                if half == 0:
                    need(pool, v_lo_done, t)
                tiles = slice(NT // 2 * half, NT // 2 * (half + 1))
                pool.wait_ge(th_done, NT * t + tiles.stop)
                for a in range(2):
                    last = nc.gpsimd.tensor_tensor(
                        wide[:, 0:NQ * 2 * E].rearrange("p (t h a e) -> p t h a e", h=HG, a=2, e=E)[:, tiles, :, a, :],
                        th[:, tiles, :].rearrange("p t (h e) -> p t h e", h=HG),
                        w_sd[:, g * HG:(g + 1) * HG, a, :].unsqueeze(1).to_broadcast([P, NT // 2, HG, E]), ALU.mult)
                last.then_inc(prod_done, 1)

            def scale_values(t):
                pool.wait_ge(factors_done, t + 1)
                pool.wait_ge(hb_done, NT * (t + 1))
                for a in range(2):
                    last = nc.gpsimd.tensor_tensor(wide_v[:, :, a * E1:(a + 1) * E1], hbq,
                                                   bb[:, :, a:a + 1].to_broadcast([P, NQ, E1]), ALU.mult)
                last.then_inc(v_done, 1)

            def low_part(t):
                pool.wait_ge(v_hi_done, t + 1)
                nc.gpsimd.tensor_tensor(v_parts[:, :, 1, :], wide_parts, v_parts[:, :, 0, :].bitcast(F32),
                                        ALU.subtract).then_inc(v_lo_done, 1)

            def join_all(t):
                pool.wait_ge(raw_all_done, NT * (t + 1))
                need(pool, rest_done, t)
                parts = raw_all[:, :, :, :, :].rearrange("p t h s e -> p (t h) s e")
                nc.gpsimd.tensor_tensor(b_all[:, :, :], parts[:, :, 0, :], parts[:, :, 1, :], ALU.add)\
                    .then_inc(b_all_done, 1)

            def add_rest(t):
                pool.wait_ge(whole_done, HG * (t + 1))
                pool.wait_ge(b_all_done, t + 1)
                nc.gpsimd.tensor_tensor(acc[:, :, 1, :], acc[:, :, 1, :], b_all[:, :, :], ALU.add)\
                    .then_inc(rest_done, 1)

            def join(t):
                pool.wait_ge(acc_done, t + 1)
                nc.gpsimd.tensor_tensor(acc[:, :, 0, :], acc[:, :, 0, :], acc[:, :, 1, :], ALU.subtract)\
                    .then_inc(joined_done, 1)

            def divide(t):
                pool.wait_ge(rden_done, t + 1)
                nc.gpsimd.tensor_tensor(acc[:, :, 0, 0:E], acc[:, :, 0, 0:E],
                                        rden[:, :].unsqueeze(2).to_broadcast([P, NQ, E]), ALU.mult)\
                    .then_inc(scaled_done, 1)

            def roots(i):
                pool.wait_ge(ve_done, i + 1)
                need(pool, norm_done, NT * i)
                nc.gpsimd.tensor_tensor(rstd[:, :], ve[:, :], half[:, :], ALU.pow).then_inc(rstd_done, 1)
                pool.wait_ge(rstd_done, i + 1)
                nc.gpsimd.tensor_tensor(shift[:, :], nmean[:, :], rstd[:, :], ALU.mult).then_inc(shift_done, 1)

            nc.gpsimd.memset(ident[:, :], 1.0).then_inc(consts_set, 1)
            pool.wait_ge(consts_set, 1)
            nc.gpsimd.affine_select(out=ident[:, :], in_=ident[:, :], compare_op=ALU.is_equal, fill=0.0, base=0,
                                    pattern=[[-1, P]], channel_multiplier=1).then_inc(ident_set, 1)
            pool.wait_ge(ident_set, 1)
            nc.gpsimd.tensor_copy(ident_b[:, :], ident[:, :]).then_inc(ident_set, 1)
            pool.wait_ge(ones_set, 1)
            pool.wait_ge(gate_bias_set, 1)
            products(0, 0, 0)
            products(0, 0, 1)
            scale_values(0)

            def batch(i, par, more):
                for g in range(GROUPS):
                    t = GROUPS * i + g
                    ahead = more or g < GROUPS - 1
                    before = not isinstance(i, int) or t > 0
                    low_part(t)
                    if before:
                        add_rest(t - 1)
                    if ahead:
                        products(t + 1, (g + 1) % GROUPS, 0)
                    if before:
                        join(t - 1)
                        divide(t - 1)
                    if ahead:
                        products(t + 1, (g + 1) % GROUPS, 1)
                        scale_values(t + 1)
                    if g == 0 and before:
                        roots(i - 1)
                    join_all(t)

            batches(pool, batch)
            last = GROUPS * B - 1
            add_rest(last)
            join(last)
            divide(last)
            roots(B - 1)


_INS = ["x", "adj", "w_all", "w_src", "w_dst", "b", "h_bias"]


def kernel(x, adj, L0_gnn_W, L0_gnn_b, L0_gnn_w_src, L0_gnn_w_dst, L0_gnn_H_w, L0_gnn_H_b):
    import numpy as _np
    import concourse.bacc as _bacc
    from concourse import mybir as _mybir
    from concourse.bass_utils import run_bass_kernel_spmd as _run

    heads, d, e = L0_gnn_W.shape
    groups = 6
    w_heads = _np.transpose(_np.asarray(L0_gnn_W), (1, 0, 2)).reshape(d, groups, -1)
    w_gate = _np.asarray(L0_gnn_H_w).T.reshape(d, groups, -1)
    laid = {
        "x": x, "adj": adj, "w_all": _np.concatenate([w_heads, w_gate], axis=2),
        "w_src": _np.asarray(L0_gnn_w_src).reshape(heads, e), "w_dst": _np.asarray(L0_gnn_w_dst).reshape(heads, e),
        "b": L0_gnn_b, "h_bias": L0_gnn_H_b,
    }
    nc = _bacc.Bacc("TRN2", target_bir_lowering=False, num_devices=1)
    arrays, args = {}, []
    for name in _INS:
        a = _np.ascontiguousarray(laid[name])
        arrays[f"in_{name}_dram"] = a
        args.append(nc.dram_tensor(f"in_{name}_dram", a.shape, _mybir.dt.from_np(a.dtype), kind="ExternalInput").ap())
    args.append(nc.dram_tensor("out_0_dram", x.shape, _mybir.dt.float32, kind="ExternalOutput").ap())
    gnn_kernel(nc, *args)
    r = _run(nc, [arrays], core_ids=[0])
    return r.results[0]["out_0_dram"]
```

```python
from contextlib import ExitStack

import concourse.bass as bass
from concourse import mybir

P = 128
F32 = mybir.dt.float32
F32R = mybir.dt.float32r
BF16 = mybir.dt.bfloat16
U8 = mybir.dt.uint8
ALU = mybir.AluOpType
ACT = mybir.ActivationFunctionType
AX_X = mybir.AxisListType.X



def gnn_kernel(nc, x, adj, w_all, w_src, w_dst, b, h_bias, out):
    B, N, D = x.shape
    GROUPS, COLS = w_all.shape[1], w_all.shape[2]
    HEADS, E = w_src.shape
    HG = HEADS // GROUPS
    HW = HG * E
    NT = N // P
    KC = D // P
    E1 = E + 1
    PAIR = 2 * E1
    QUAD = 4 * E1
    SLOPE = 0.2
    EPS = 1e-5
    NQ = NT * HG
    SUMS = NT * HG
    RING = 3
    GATES = 3
    assert COLS == 2 * HW and QUAD <= 512 and N == 512 and GROUPS == 6 and HG == 2 and KC == 6
    ADJ_STEP, X_STEP = 3, 4
    P_AT = [0, NT, 2 * NT, 3 * NT, 5 * NT, 6 * NT + KC]
    ADJ_AT, X_AT = 4 * NT, 6 * NT
    UNITS = GROUPS * NT + KC + NT
    FIRST_UNITS = KC + NT + NT

    ctx = ExitStack()
    with ctx:
        def sb(name, shape, dt):
            return ctx.enter_context(nc.sbuf_tensor(name, shape, dt))

        def ps(name, shape, dt):
            return ctx.enter_context(nc.psum_tensor(name, shape, dt))

        def sem(name):
            return ctx.enter_context(nc.semaphore(name))

        w_hi = sb("w_hi", [P, KC, GROUPS, COLS], F32R)
        w_lo = sb("w_lo", [P, KC, GROUPS, COLS], F32R)
        xt_hi = sb("xt_hi", [P, KC, N], F32R)
        xt_lo = sb("xt_lo", [P, KC, N], F32R)
        xy = sb("xy", [P, 2, NT, D], F32)
        sel = sb("sel", [P, HG, NT, N], F32R)
        nadj = sb("nadj", [P, 2, NT, N], F32R)
        hb = sb("hb", [P, NT, HG, E1], F32)
        th = sb("th", [P, NT, HW], F32)
        gate = sb("gate", [P, GATES, NT, HW], F32)
        wide = sb("wide", [P, NQ * PAIR], F32)
        v = sb("v", [P, NQ, 4, E1], F32R)
        raw = sb("raw", [P, NT, HG, 4, E1], F32)
        raw_all = sb("raw_all", [P, NT, HG, 2, E1], F32)
        b_all = sb("b_all", [P, NQ, E1], F32)
        acc = sb("acc", [P, NQ, 2, E1], F32)
        adj8 = sb("adj8", [P, NT, N], U8)
        adjb = sb("adjb", [P, 2, N], BF16)
        w_sd = sb("w_sd", [P, HEADS, 2, E], F32)
        bias1 = sb("bias1", [P, E], F32)
        d_bound = sb("d_bound", [P, HEADS], F32)
        hb3 = sb("hb3", [P, D], BF16)
        ones_b = sb("ones_b", [P, 2], BF16)
        ident = sb("ident", [P, P], F32)
        ident_b = sb("ident_b", [P, P], BF16)
        minus1 = sb("minus1", [P, 1], F32)
        half = sb("half", [P, NT], F32)
        sd = sb("sd", [P, 2, NQ, 2], F32)
        sdb = sb("sdb", [P, NQ, 2], F32)
        log_rho = sb("log_rho", [P, NQ], F32)
        rho = sb("rho", [P, 2, NQ], F32)
        bb = sb("bb", [P, NQ, 2], F32)
        rden = sb("rden", [P, NQ], F32)
        stats = sb("stats", [P, NT, GROUPS, 6], F32)
        mv = sb("mv", [P, NT, 2], F32)
        ve = sb("ve", [P, NT], F32)
        nmean = sb("nmean", [P, NT], F32)
        rstd = sb("rstd", [P, NT], F32)
        shift = sb("shift", [P, NT], F32)

        work = ps("work", [P, 2, 512], F32)
        s_row = ps("s_row", [P, 2, N], F32)
        head_sum = ps("head_sum", [P, RING, 512], F32)
        all_sum = ps("all_sum", [P, 1, 512], F32)

        w_in = [sem(f"w_in{k}") for k in range(KC)]
        small_in = sem("small_in")
        gate_bias_in = sem("gate_bias_in")
        ones_set = sem("ones_set")
        ident_set = sem("ident_set")
        consts_set = sem("consts_set")
        gate_bias_set = sem("gate_bias_set")
        w_split_hi = sem("w_split_hi")
        w_split_lo = sem("w_split_lo")
        gate_bias_halved = sem("gate_bias_halved")
        w_sd_set = sem("w_sd_set")
        abs_set = sem("abs_set")
        x_in = [sem("x_in0"), sem("x_in1")]
        adj_in = sem("adj_in")
        stored = [sem("stored0"), sem("stored1")]
        unit_full = sem("unit_full")
        s_row_full = sem("s_row_full")
        all_sum_full = sem("all_sum_full")
        head_sum_full = sem("head_sum_full")
        th_done = sem("th_done")
        xt_hi_done = sem("xt_hi_done")
        adjb_done = sem("adjb_done")
        nadj_done = sem("nadj_done")
        factors_done = sem("factors_done")
        v_hi_done = sem("v_hi_done")
        exp_done = sem("exp_done")
        raw_done = sem("raw_done")
        raw_all_done = sem("raw_all_done")
        norm_done = sem("norm_done")
        xt_lo_done = sem("xt_lo_done")
        sd_done = sem("sd_done")
        sdb_done = sem("sdb_done")
        log_rho_done = sem("log_rho_done")
        sel_done = sem("sel_done")
        whole_done = sem("whole_done")
        rest_done = sem("rest_done")
        acc_done = sem("acc_done")
        rden_done = sem("rden_done")
        elu_done = sem("elu_done")
        diff_done = sem("diff_done")
        gated_done = sem("gated_done")
        y_done = sem("y_done")
        stats_done = sem("stats_done")
        mv_done = sem("mv_done")
        ve_done = sem("ve_done")
        prod_done = sem("prod_done")
        hb_done = sem("hb_done")
        v_done = sem("v_done")
        v_lo_done = sem("v_lo_done")
        b_all_done = sem("b_all_done")
        joined_done = sem("joined_done")
        scaled_done = sem("scaled_done")
        rstd_done = sem("rstd_done")
        shift_done = sem("shift_done")

        x_v = x.rearrange("b (t p) d -> b p t d", p=P)
        out_v = out.rearrange("b (t p) d -> b p t d", p=P)
        adj_v = adj.rearrange("b p n -> (b p n)")
        w_v = w_all.rearrange("(k p) g c -> k p (g c)", p=P)

        def need(eng, s, count):
            if not isinstance(count, int) or count > 0:
                eng.wait_ge(s, count)

        def units(i, j):
            return FIRST_UNITS + UNITS * i + j + 1

        def first_unit(g, more):
            return P_AT[g] if more or g < ADJ_STEP + 1 else ADJ_AT

        def batches(eng, body):
            body(0, 0, True)
            body(1, 1, True)
            with eng.Fori(2, B - 2, 2) as i:
                body(i, 0, True)
                body(i + 1, 1, True)
            body(B - 2, 0, True)
            body(B - 1, 1, False)

        prod_v = wide[:, 0:NQ * 2 * E].rearrange("p (q e) -> p q e", e=E)
        wide_v = wide[:, :].rearrange("p (q e) -> p q e", e=PAIR)
        hbq = hb[:, :, :, :].rearrange("p t h e -> p (t h) e")
        v_parts = v[:, :, :, :].rearrange("p q (a s) e -> p (q a) s e", s=2)
        wide_parts = wide[:, :].rearrange("p (q e) -> p q e", e=E1)
        w_stage = [xy[:, 1, 0:2, :].rearrange("p t d -> p (t d)"), xy[:, 1, 2:4, :].rearrange("p t d -> p (t d)"),
                   gate[:, :, :, :].rearrange("p g t c -> p (g t c)"),
                   raw[:, :, :, :, :].rearrange("p t h s e -> p (t h s e)")[:, 0:GROUPS * COLS]]
        STAGES = len(w_stage)
        abs_stage = wide[:, 0:D]
        hb_stage = acc[:, :, :, :].rearrange("p q a e -> p (q a e)")[:, 0:D]
        hb_part = b_all[:, :, :].rearrange("p q e -> p (q e)").bitcast(BF16)[:, 0:D]

        block = ctx.enter_context(nc.Block())

        @block.sync
        def _(sp):
            def load_adj(i):
                start = NT * i * P * N
                if not isinstance(i, int):
                    start = sp.snap(start)
                rows = adj_v[bass.ds(start, N * N)].rearrange("(t p n) -> p t n", p=P, n=N)
                need(sp, adjb_done, NT * i)
                sp.dma_start(adj8[:, :, :], rows).then_inc(adj_in, 16)

            sp.dma_start(hb_stage, h_bias.partition_broadcast(P)).then_inc(gate_bias_in, 16)
            sp.dma_start(xy[:, 0], x_v[0]).then_inc(x_in[0], 16)
            load_adj(0)
            sp.dma_start(w_sd[:, :, 0, :], w_src.partition_broadcast(P)).then_inc(small_in, 16)
            sp.dma_start(w_sd[:, :, 1, :], w_dst.partition_broadcast(P)).then_inc(small_in, 16)
            sp.dma_start(bias1[:, :], b.partition_broadcast(P)).then_inc(small_in, 16)
            for k in range(KC):
                need(sp, w_split_lo, 2 * (k - STAGES + 1))
                sp.dma_start(w_stage[k % STAGES], w_v[k]).then_inc(w_in[k], 16)
            sp.wait_ge(w_split_lo, 2 * KC)
            sp.dma_start(xy[:, 1], x_v[1]).then_inc(x_in[1], 16)

            def batch(i, par, more):
                if more:
                    load_adj(i + 1)
                if not (isinstance(i, int) and i == 0):
                    sp.wait_ge(norm_done, NT * i)
                    sp.dma_start(out_v[i - 1], xy[:, 1 - par]).then_inc(stored[1 - par], 16)
                    if more:
                        sp.wait_ge(stored[1 - par], 8 * (i + par))
                        sp.dma_start(xy[:, 1 - par], x_v[i + 1]).then_inc(x_in[1 - par], 16)

            batches(sp, batch)
            for n in range(NT):
                sp.wait_ge(norm_done, NT * (B - 1) + n + 1)
                sp.dma_start(out_v[B - 1][:, n, :], xy[:, (B - 1) % 2, n, :]).then_inc(stored[(B - 1) % 2], 16)
            sp.wait_ge(stored[0], 16 * (B // 2))
            sp.wait_ge(stored[1], 16 * (B // 2 - 1 + NT))

        @block.tensor
        def _(pe):
            def release(i, j, more):
                j -= 2
                if j < 0:
                    i, j, more = i - 1, j + UNITS, True
                if j < ADJ_AT or not more:
                    pe.wait_ge(th_done, GROUPS * NT * i + NT + j + 1)
                elif j < P_AT[4]:
                    pe.wait_ge(nadj_done, NT * (i + 1) + j - ADJ_AT + 1)
                elif j < X_AT:
                    pe.wait_ge(th_done, GROUPS * NT * i + NT + j - NT + 1)
                elif j < P_AT[5]:
                    pe.wait_ge(xt_lo_done, KC * (i + 1) + j - X_AT + 1)
                else:
                    pe.wait_ge(th_done, GROUPS * NT * (i + 1) + j - P_AT[5] + 1)

            def transpose_x(i, k, bank):
                for t in range(NT):
                    mm = pe.transpose(work[:, bank, t * P:(t + 1) * P], xy[:, i, t, k * P:(k + 1) * P], ident[:, :])
                mm.then_inc(unit_full, 1)

            def transpose_adj(t, bank):
                dst = work[:, bank, :].bitcast(BF16)
                for m in range(NT):
                    mm = pe.transpose(dst[:, m * P:(m + 1) * P], adjb[:, t % 2, m * P:(m + 1) * P], ident_b[:, :])
                mm.then_inc(unit_full, 1)

            def project(g, m, bank):
                dst = work[:, bank, 0:COLS]
                for k in range(KC):
                    xh, xl = xt_hi[:, k, m * P:(m + 1) * P], xt_lo[:, k, m * P:(m + 1) * P]
                    pe.matmul(dst, xh, w_hi[:, k, g, :], start=(k == 0), stop=False, skip_group_check=True)
                    pe.matmul(dst, xh, w_lo[:, k, g, :], start=False, stop=False, skip_group_check=True)
                    pe.matmul(dst, xl, w_hi[:, k, g, :], start=False, stop=False, skip_group_check=True)
                pe.matmul(work[:, bank, HW:COLS], ones_b[:, 0:1].to_broadcast([P, P]), hb3[:, g * HW:(g + 1) * HW],
                          start=False, stop=True, skip_group_check=True).then_inc(unit_full, 1)

            def spread_s(t, par, h):
                need(pe, sel_done, HG * (t - 1) + h + 1)
                for m in range(NT):
                    mm = pe.transpose(s_row[:, h, m * P:(m + 1) * P],
                                      sd[:, par, m * HG + h, 0:1].to_broadcast([P, P]), ident[:, :])
                mm.then_inc(s_row_full, 1)

            def sum_all(i, t, par, n):
                need(pe, raw_all_done, NT * t + n)
                for m in range(NT):
                    mm = pe.matmul(all_sum[:, 0, 0:QUAD], nadj[:, par, m, n * P:(n + 1) * P],
                                   v[:, m * HG:(m + 1) * HG, 2:4, :].rearrange("p h s e -> p h (s e)"),
                                   start=(m == 0), stop=(m == NT - 1))
                mm.then_inc(all_sum_full, 1)

            def sum_head(t, g, h, n):
                c = NT * h + n
                need(pe, raw_done, SUMS * t + c - RING + 1)
                for m in range(NT):
                    mm = pe.matmul(head_sum[:, (SUMS * g + c) % RING, 0:QUAD], sel[:, h, m, n * P:(n + 1) * P],
                                   v[:, m * HG + h, :, :].rearrange("p s e -> p (s e)"),
                                   start=(m == 0), stop=(m == NT - 1))
                mm.then_inc(head_sum_full, 1)

            pe.wait_ge(ident_set, 2)
            pe.wait_ge(x_in[0], 16)
            for k in range(KC):
                need(pe, xt_lo_done, k - 1)
                transpose_x(0, k, k % 2)
            for t in range(NT):
                if t < 2:
                    pe.wait_ge(xt_lo_done, KC - 1 + t)
                else:
                    pe.wait_ge(nadj_done, t - 1)
                pe.wait_ge(adjb_done, t + 1)
                transpose_adj(t, t % 2)
            pe.wait_ge(w_split_lo, 2 * KC)
            pe.wait_ge(gate_bias_set, 8)
            for m in range(NT):
                if m < 2:
                    pe.wait_ge(nadj_done, NT - 1 + m)
                else:
                    pe.wait_ge(th_done, m - 1)
                project(0, m, m % 2)
            pe.wait_ge(sd_done, 1)
            for h in range(HG):
                spread_s(0, 0, h)

            def batch(i, par, more):
                for g in range(GROUPS):
                    t = GROUPS * i + g
                    ahead = more or g < GROUPS - 1

                    def project_ahead(m):
                        if ahead:
                            if g == GROUPS - 1 and m == 0:
                                pe.wait_ge(xt_lo_done, KC * (i + 2))
                            release(i, first_unit(g, more) + m, more)
                            project((g + 1) % GROUPS, m, m % 2)

                    for m in range(NT):
                        project_ahead(m)
                    pe.wait_ge(v_lo_done, t + 1)
                    if g == 0:
                        pe.wait_ge(nadj_done, NT * (i + 1))
                    for h in range(HG):
                        for n in range(NT):
                            c = NT * h + n
                            if c % 2 == 0:
                                sum_all(i, t, par, c // 2)
                            if n == 0:
                                pe.wait_ge(sel_done, HG * t + h + 1)
                            sum_head(t, g, h, n)
                            if ahead and c >= 6:
                                if c == 6:
                                    pe.wait_ge(sd_done, t + 2)
                                spread_s(t + 1, (g + 1) % 2, c - 6)
                            if more and g == ADJ_STEP and c % 2 == 1:
                                k = c // 2
                                pe.wait_ge(adjb_done, NT * (i + 1) + k + 1)
                                release(i, ADJ_AT + k, more)
                                transpose_adj(k, k % 2)
                            if more and g == X_STEP and c < KC:
                                k = c
                                if k == 0:
                                    pe.wait_ge(x_in[1 - par], 8 * (i + 2 + par))
                                release(i, X_AT + k, more)
                                transpose_x(1 - par, k, k % 2)

            batches(pe, batch)

        @block.scalar
        def _(act):
            def xt_high(k, count, bank):
                act.wait_ge(unit_full, count)
                nc.scalar.activation(xt_hi[:, k, :], work[:, bank, :], ACT.Copy).then_inc(xt_hi_done, 1)

            def tanhs(t, g, m, count, bank):
                act.wait_ge(unit_full, count)
                if m == 0:
                    need(act, prod_done, 2 * t)
                    need(act, y_done, t - GATES + 1)
                    need(act, v_done, t)
                nc.scalar.activation(th[:, m, :], work[:, bank, 0:HW], ACT.Tanh)
                nc.scalar.activation(hb[:, m, :, 0:E], work[:, bank, 0:HW].rearrange("p (h e) -> p h e", h=HG),
                                     ACT.Copy)
                nc.scalar.activation(gate[:, g % GATES, m, :], work[:, bank, HW:COLS], ACT.Tanh).then_inc(th_done, 1)

            def cast_adj(i, t):
                act.wait_ge(adj_in, 16 * (i + 1))
                need(act, unit_full, units(i - 1, ADJ_AT + t - 2) if t >= 2 else 0)
                nc.scalar.activation(adjb[:, t % 2, :], adj8[:, t, :], ACT.Copy, scale=-1.0).then_inc(adjb_done, 1)

            def mask(t, par, count, bank):
                act.wait_ge(unit_full, count)
                src = work[:, bank, :].bitcast(BF16)[:, 0:N].rearrange("p (m n) -> p m n", m=NT)
                nc.scalar.activation(nadj[:, par, :, t * P:(t + 1) * P], src, ACT.Copy).then_inc(nadj_done, 1)

            def factors(t, par):
                act.wait_ge(log_rho_done, t + 1)
                need(act, v_done, t)
                need(act, acc_done, t - 1)
                nc.scalar.activation(rho[:, par, :], log_rho[:, :], ACT.Exp)
                nc.scalar.activation(bb[:, :, 0], sdb[:, :, 1], ACT.Exp, scale=-1.0)
                nc.scalar.activation(bb[:, :, 1], sdb[:, :, 1], ACT.Exp, scale=-SLOPE).then_inc(factors_done, 1)

            for k in range(KC):
                xt_high(k, k + 1, k % 2)
            cast_adj(0, 0)
            cast_adj(0, 1)
            for t in range(NT):
                mask(t, 0, KC + t + 1, t % 2)
                if t < NT - 2:
                    cast_adj(0, t + 2)
            for k in range(KC):
                act.wait_ge(w_in[k], 16)
                src = w_stage[k % STAGES].rearrange("p (g c) -> p g c", g=GROUPS)
                nc.scalar.activation(w_hi[:, k, :, 0:HW], src[:, :, 0:HW], ACT.Copy)
                nc.scalar.activation(w_hi[:, k, :, HW:COLS], src[:, :, HW:COLS], ACT.Copy, scale=0.5)\
                    .then_inc(w_split_hi, 1)
            for m in range(NT):
                tanhs(0, 0, m, KC + NT + m + 1, m % 2)
            factors(0, 0)

            def v_high(t):
                act.wait_ge(v_done, t + 1)
                need(act, head_sum_full, SUMS * t)
                nc.scalar.activation(v_parts[:, :, 0, :], wide_parts, ACT.Copy).then_inc(v_hi_done, 1)

            def read_all(t, n):
                act.wait_ge(all_sum_full, NT * t + n + 1)
                if n == 0:
                    need(act, b_all_done, t)
                nc.scalar.activation(raw_all[:, n, :, :, :].rearrange("p h s e -> p (h s e)"),
                                     all_sum[:, 0, 0:QUAD], ACT.Copy).then_inc(raw_all_done, 1)

            def read_head(t, g, c):
                h, n = c // NT, c % NT
                act.wait_ge(head_sum_full, SUMS * t + c + 1)
                if n == 0:
                    need(act, whole_done, HG * (t - 1) + h + 1)
                nc.scalar.activation(raw[:, n, h, :, :].rearrange("p s e -> p (s e)"),
                                     head_sum[:, (SUMS * g + c) % RING, 0:QUAD], ACT.Copy).then_inc(raw_done, 1)

            def batch(i, par, more):
                for g in range(GROUPS):
                    t = GROUPS * i + g
                    ahead = more or g < GROUPS - 1
                    before = not isinstance(i, int) or t > 0
                    v_high(t)
                    for m in range(NT):
                        if g == 2 and not (isinstance(i, int) and i == 0):
                            normalise(i - 1, 1 - par, m)
                        if m == 3 and before:
                            exp_values(t - 1)
                        if ahead:
                            tanhs(t + 1, (g + 1) % GROUPS, m, units(i, first_unit(g, more) + m), m % 2)
                        if more and g == ADJ_STEP and m < 2:
                            cast_adj(i + 1, m)
                    for c in range(SUMS):
                        if c % 2 == 0:
                            read_all(t, c // 2)
                        read_head(t, g, c)
                        if more and g == ADJ_STEP and (c in (2, 4, 6) or c == 7):
                            n = (c - 1) // 2
                            mask(n, 1 - par, units(i, ADJ_AT + n), n % 2)
                            if n < NT - 2:
                                cast_adj(i + 1, n + 2)
                        if more and g == X_STEP and c < KC:
                            xt_high(c, units(i, X_AT + c), c % 2)
                        if c == 4 and ahead:
                            factors(t + 1, (g + 1) % 2)

            def exp_values(t):
                act.wait_ge(scaled_done, t + 1)
                nc.scalar.activation(acc[:, :, 1, 0:E], acc[:, :, 0, 0:E], ACT.Exp, bias=minus1[:, 0:1])\
                    .then_inc(exp_done, 1)

            def normalise(i, par, n):
                act.wait_ge(shift_done, i + 1)
                nc.scalar.activation(xy[:, par, n, :], xy[:, par, n, :], ACT.Identity, bias=shift[:, n:n + 1],
                                     scale=rstd[:, n:n + 1]).then_inc(norm_done, 1)

            batches(act, batch)
            exp_values(GROUPS * B - 1)
            for n in range(NT):
                normalise(B - 1, (B - 1) % 2, n)

        @block.vector
        def _(dve):
            def xt_low(k, count, bank):
                dve.wait_ge(xt_hi_done, count)
                nc.vector.tensor_tensor(xt_lo[:, k, :], work[:, bank, :], xt_hi[:, k, :].bitcast(F32), ALU.subtract)\
                    .then_inc(xt_lo_done, 1)

            def add_up(t, par, half):
                dve.wait_ge(prod_done, 2 * t + half + 1)
                qs = slice(NQ * half, NQ * (half + 1))
                last = nc.vector.tensor_reduce(sd[:, par, :, :].rearrange("p q a -> p (q a)")[:, qs], prod_v[:, qs, :],
                                               AX_X, ALU.add)
                if half == 1:
                    last.then_inc(sd_done, 1)

            def terms(t, g, par):
                dve.wait_ge(sd_done, t + 1)
                need(dve, factors_done, t)
                bound = d_bound[:, g * HG:(g + 1) * HG].unsqueeze(1).unsqueeze(3).to_broadcast([P, NT, HG, 2])
                nc.vector.tensor_tensor(sdb[:, :, :].rearrange("p (t h) a -> p t h a", t=NT),
                                        sd[:, par, :, :].rearrange("p (t h) a -> p t h a", t=NT), bound, ALU.add)\
                    .then_inc(sdb_done, 1)
                dve.wait_ge(sdb_done, t + 1)
                nc.vector.tensor_scalar(log_rho[:, :], sdb[:, :, 0], SLOPE - 1.0, 0.0, ALU.mult, ALU.min)\
                    .then_inc(log_rho_done, 1)

            def select(t, par, mpar, h, tiles):
                if tiles[0] == 0:
                    dve.wait_ge(s_row_full, HG * t + h + 1)
                    need(dve, head_sum_full, SUMS * (t - 1) + NT * (h + 1))
                for m in tiles:
                    last = nc.vector.scalar_tensor_tensor(out=sel[:, h, m, :], in0=s_row[:, h, :],
                                                          scalar=sd[:, par, m * HG + h, 1:2],
                                                          in1=nadj[:, mpar, m, :].bitcast(F32),
                                                          op0=ALU.is_ge, op1=ALU.logical_and)
                if tiles[-1] == NT - 1:
                    last.then_inc(sel_done, 1)

            def whole(t, h):
                dve.wait_ge(raw_done, SUMS * t + NT * (h + 1))
                need(dve, y_done, t)
                parts = raw[:, :, h, :, :].rearrange("p t (a s) e -> p t a s e", s=2)
                nc.vector.tensor_tensor(acc[:, :, :, :].rearrange("p (t h) a e -> p t h a e", t=NT)[:, :, h, :, :],
                                        parts[:, :, :, 0, :], parts[:, :, :, 1, :], ALU.add).then_inc(whole_done, 1)

            def add_rest(t):
                dve.wait_ge(whole_done, HG * (t + 1))
                dve.wait_ge(b_all_done, t + 1)
                nc.vector.tensor_tensor(acc[:, :, 1, :], acc[:, :, 1, :], b_all[:, :, :], ALU.add)\
                    .then_inc(rest_done, 1)

            def weigh(t, par):
                dve.wait_ge(rest_done, t + 1)
                nc.vector.tensor_tensor(acc[:, :, 1, :], acc[:, :, 1, :],
                                        rho[:, par, :].unsqueeze(2).to_broadcast([P, NQ, E1]), ALU.mult)\
                    .then_inc(acc_done, 1)

            def invert(t):
                dve.wait_ge(joined_done, t + 1)
                nc.vector.reciprocal(rden[:, :], acc[:, :, 0, E]).then_inc(rden_done, 1)

            def elu(t, g, xpar):
                f = acc[:, :, 1, 0:E]
                dve.wait_ge(exp_done, t + 1)
                nc.vector.scalar_tensor_tensor(out=f, in0=f, scalar=1.0, in1=acc[:, :, 0, 0:E],
                                               op0=ALU.min, op1=ALU.max).then_inc(elu_done, 1)
                dve.wait_ge(elu_done, t + 1)
                xg = xy[:, xpar, :, g * HW:(g + 1) * HW]
                nc.vector.scalar_tensor_tensor(out=f.rearrange("p (t h) e -> p t h e", t=NT),
                                               in0=f.rearrange("p (t h) e -> p t h e", t=NT), scalar=1.0,
                                               in1=xg.rearrange("p t (h e) -> p t h e", h=HG),
                                               op0=ALU.subtract, op1=ALU.subtract).then_inc(diff_done, 1)

            def mix(t, g, xpar):
                f = acc[:, :, 1, 0:E].rearrange("p (t h) e -> p t h e", t=NT)
                xg = xy[:, xpar, :, g * HW:(g + 1) * HW].rearrange("p t (h e) -> p t h e", h=HG)
                dve.wait_ge(diff_done, t + 1)
                nc.vector.scalar_tensor_tensor(out=f, scalar=1.0,
                                               in0=gate[:, g % GATES, :, :].rearrange("p t (h e) -> p t h e", h=HG),
                                               in1=f, op0=ALU.add, op1=ALU.mult).then_inc(gated_done, 1)
                dve.wait_ge(gated_done, t + 1)
                nc.vector.scalar_tensor_tensor(out=xg, in0=xg, scalar=4.0, in1=f, op0=ALU.mult, op1=ALU.add)\
                    .then_inc(y_done, 1)

            def moments(t, g, xpar):
                dve.wait_ge(y_done, t + 1)
                for n in range(NT):
                    last = nc.vector.bn_stats(stats[:, n, g, :], xy[:, xpar, n, g * HW:(g + 1) * HW])
                if g == GROUPS - 1:
                    last.then_inc(stats_done, 1)

            def row_moments(i):
                need(dve, shift_done, i)
                dve.wait_ge(stats_done, i + 1)
                nc.vector.memset(nmean[:, :], 0.0)
                for n in range(NT):
                    last = nc.vector.bn_aggr(mv[:, n, :], stats[:, n, :, :].rearrange("p c s -> p (c s)"))
                last.then_inc(mv_done, 1)
                dve.wait_ge(mv_done, i + 1)
                nc.vector.tensor_scalar(ve[:, :], mv[:, :, 1], 4.0 * EPS, None, ALU.add)
                nc.vector.tensor_scalar(nmean[:, :], mv[:, :, 0], -1.0, None, ALU.mult).then_inc(ve_done, 1)

            nc.vector.memset(hb[:, :, :, E:E + 1], 1.0)
            nc.vector.memset(minus1[:, :], -1.0)
            nc.vector.memset(half[:, :], -0.5)
            nc.vector.memset(ones_b[:, :], 1.0)
            nc.vector.memset(hb3[:, :], 0.0).then_inc(ones_set, 1)
            dve.wait_ge(gate_bias_in, 16)
            nc.vector.tensor_scalar(hb_stage, hb_stage, 0.5, None, ALU.mult).then_inc(gate_bias_halved, 1)
            for k in range(KC):
                xt_low(k, k + 1, k % 2)
            dve.wait_ge(small_in, 48)
            dve.wait_ge(ones_set, 1)

            nc.vector.tensor_scalar(bias1[:, :], bias1[:, :], 1.0, None, ALU.add)
            nc.vector.scalar_tensor_tensor(out=abs_stage.rearrange("p (h e) -> p h e", h=HEADS),
                                           in0=w_sd[:, :, 1, :], scalar=-1.0, in1=w_sd[:, :, 1, :],
                                           op0=ALU.mult, op1=ALU.max).then_inc(abs_set, 1)
            dve.wait_ge(abs_set, 1)
            nc.vector.tensor_reduce(d_bound[:, :], abs_stage.rearrange("p (h e) -> p h e", h=HEADS), AX_X, ALU.add)
            nc.vector.tensor_scalar(w_sd[:, :, 1, :], w_sd[:, :, 1, :], -1.0, None, ALU.mult)\
                .then_inc(w_sd_set, 1)
            for k in range(KC):
                dve.wait_ge(w_split_hi, k + 1)
                src = w_stage[k % STAGES].rearrange("p (g c) -> p g c", g=GROUPS)
                nc.vector.tensor_tensor(w_lo[:, k, :, 0:HW], src[:, :, 0:HW], w_hi[:, k, :, 0:HW].bitcast(F32),
                                        ALU.subtract).then_inc(w_split_lo, 1)
                nc.vector.scalar_tensor_tensor(out=w_lo[:, k, :, HW:COLS], in0=src[:, :, HW:COLS], scalar=0.5,
                                               in1=w_hi[:, k, :, HW:COLS].bitcast(F32), op0=ALU.mult,
                                               op1=ALU.subtract).then_inc(w_split_lo, 1)
            add_up(0, 0, 0)
            add_up(0, 0, 1)
            terms(0, 0, 0)

            def batch(i, par, more):
                later = not (isinstance(i, int) and i == 0)
                for g in range(GROUPS):
                    t = GROUPS * i + g
                    ahead = more or g < GROUPS - 1
                    before = later or g > 0
                    gb, xb = (g - 1) % GROUPS, (par if g else 1 - par)
                    if g == 0:
                        dve.wait_ge(nadj_done, NT * (i + 1))
                    select(t, g % 2, par, 0, [0])
                    if before:
                        add_rest(t - 1)
                        weigh(t - 1, (g + 1) % 2)
                    select(t, g % 2, par, 0, [1, 2, 3])
                    if before:
                        invert(t - 1)
                    select(t, g % 2, par, 1, [0, 1, 2, 3])
                    if later and g == 1:
                        row_moments(i - 1)
                    if ahead:
                        add_up(t + 1, (g + 1) % 2, 0)
                    if before:
                        elu(t - 1, gb, xb)
                    if more and g == X_STEP:
                        for k in range(0, 3):
                            xt_low(k, KC * (i + 1) + k + 1, k % 2)
                    if ahead:
                        add_up(t + 1, (g + 1) % 2, 1)
                        terms(t + 1, (g + 1) % GROUPS, (g + 1) % 2)
                    if more and g == X_STEP:
                        for k in range(3, 6):
                            xt_low(k, KC * (i + 1) + k + 1, k % 2)
                    if before:
                        mix(t - 1, gb, xb)
                        moments(t - 1, gb, xb)
                    whole(t, 0)
                    whole(t, 1)

            batches(dve, batch)
            last = GROUPS * B - 1
            add_rest(last)
            weigh(last, 1)
            invert(last)
            elu(last, GROUPS - 1, (B - 1) % 2)
            mix(last, GROUPS - 1, (B - 1) % 2)
            moments(last, GROUPS - 1, (B - 1) % 2)
            row_moments(B - 1)

        @block.gpsimd
        def _(pool):
            def products(t, g, half):
                if half == 0:
                    need(pool, v_lo_done, t)
                tiles = slice(NT // 2 * half, NT // 2 * (half + 1))
                pool.wait_ge(th_done, NT * t + tiles.stop)
                for a in range(2):
                    last = nc.gpsimd.tensor_tensor(
                        wide[:, 0:NQ * 2 * E].rearrange("p (t h a e) -> p t h a e", h=HG, a=2, e=E)[:, tiles, :, a, :],
                        th[:, tiles, :].rearrange("p t (h e) -> p t h e", h=HG),
                        w_sd[:, g * HG:(g + 1) * HG, a, :].unsqueeze(1).to_broadcast([P, NT // 2, HG, E]), ALU.mult)
                last.then_inc(prod_done, 1)

            def add_bias(t):
                pool.wait_ge(th_done, NT * (t + 1))
                nc.gpsimd.tensor_tensor(hb[:, :, :, 0:E].rearrange("p t h e -> p (t h) e"),
                                        hb[:, :, :, 0:E].rearrange("p t h e -> p (t h) e"),
                                        bias1[:, :].unsqueeze(1).to_broadcast([P, NQ, E]), ALU.add)\
                    .then_inc(hb_done, 1)

            def scale_values(t):
                pool.wait_ge(factors_done, t + 1)
                pool.wait_ge(hb_done, t + 1)
                for a in range(2):
                    last = nc.gpsimd.tensor_tensor(wide_v[:, :, a * E1:(a + 1) * E1], hbq,
                                                   bb[:, :, a:a + 1].to_broadcast([P, NQ, E1]), ALU.mult)
                last.then_inc(v_done, 1)

            def low_part(t):
                pool.wait_ge(v_hi_done, t + 1)
                nc.gpsimd.tensor_tensor(v_parts[:, :, 1, :], wide_parts, v_parts[:, :, 0, :].bitcast(F32),
                                        ALU.subtract).then_inc(v_lo_done, 1)

            def join_all(t):
                pool.wait_ge(raw_all_done, NT * (t + 1))
                need(pool, rest_done, t)
                parts = raw_all[:, :, :, :, :].rearrange("p t h s e -> p (t h) s e")
                nc.gpsimd.tensor_tensor(b_all[:, :, :], parts[:, :, 0, :], parts[:, :, 1, :], ALU.add)\
                    .then_inc(b_all_done, 1)

            def join(t):
                pool.wait_ge(acc_done, t + 1)
                nc.gpsimd.tensor_tensor(acc[:, :, 0, :], acc[:, :, 0, :], acc[:, :, 1, :], ALU.subtract)\
                    .then_inc(joined_done, 1)

            def divide(t):
                pool.wait_ge(rden_done, t + 1)
                nc.gpsimd.tensor_tensor(acc[:, :, 0, 0:E], acc[:, :, 0, 0:E],
                                        rden[:, :].unsqueeze(2).to_broadcast([P, NQ, E]), ALU.mult)\
                    .then_inc(scaled_done, 1)

            def roots(i):
                pool.wait_ge(ve_done, i + 1)
                need(pool, norm_done, NT * i)
                nc.gpsimd.tensor_tensor(rstd[:, :], ve[:, :], half[:, :], ALU.pow).then_inc(rstd_done, 1)
                pool.wait_ge(rstd_done, i + 1)
                nc.gpsimd.tensor_tensor(shift[:, :], nmean[:, :], rstd[:, :], ALU.mult).then_inc(shift_done, 1)

            nc.gpsimd.memset(ident[:, :], 1.0).then_inc(consts_set, 1)
            pool.wait_ge(consts_set, 1)
            nc.gpsimd.affine_select(out=ident[:, :], in_=ident[:, :], compare_op=ALU.is_equal, fill=0.0, base=0,
                                    pattern=[[-1, P]], channel_multiplier=1).then_inc(ident_set, 1)
            pool.wait_ge(ident_set, 1)
            nc.gpsimd.tensor_copy(ident_b[:, :], ident[:, :]).then_inc(ident_set, 1)
            pool.wait_ge(ones_set, 1)
            pool.wait_ge(gate_bias_halved, 1)
            for j in range(3):
                rows = slice(32 * j, 32 * j + 1)
                nc.gpsimd.tensor_copy(hb_part, hb_stage).then_inc(gate_bias_set, 1)
                pool.wait_ge(gate_bias_set, 3 * j + 1)
                nc.gpsimd.tensor_copy(hb3[rows, :], hb_part[rows, :]).then_inc(gate_bias_set, 1)
                pool.wait_ge(gate_bias_set, 3 * j + 2)
                if j < 2:
                    nc.gpsimd.tensor_tensor(hb_stage, hb_stage, hb_part, ALU.subtract).then_inc(gate_bias_set, 1)
                    pool.wait_ge(gate_bias_set, 3 * j + 3)
            pool.wait_ge(w_sd_set, 1)
            products(0, 0, 0)
            products(0, 0, 1)
            add_bias(0)
            scale_values(0)

            def batch(i, par, more):
                for g in range(GROUPS):
                    t = GROUPS * i + g
                    ahead = more or g < GROUPS - 1
                    before = not isinstance(i, int) or t > 0
                    low_part(t)
                    if before:
                        join(t - 1)
                        divide(t - 1)
                    if ahead:
                        products(t + 1, (g + 1) % GROUPS, 0)
                        products(t + 1, (g + 1) % GROUPS, 1)
                        add_bias(t + 1)
                    if g == 1 and not (isinstance(i, int) and i == 0):
                        roots(i - 1)
                    if ahead:
                        scale_values(t + 1)
                    join_all(t)

            batches(pool, batch)
            last = GROUPS * B - 1
            join(last)
            divide(last)
            roots(B - 1)


_INS = ["x", "adj", "w_all", "w_src", "w_dst", "b", "h_bias"]


def kernel(x, adj, L0_gnn_W, L0_gnn_b, L0_gnn_w_src, L0_gnn_w_dst, L0_gnn_H_w, L0_gnn_H_b):
    import numpy as _np
    import concourse.bacc as _bacc
    from concourse import mybir as _mybir
    from concourse.bass_utils import run_bass_kernel_spmd as _run

    heads, d, e = L0_gnn_W.shape
    groups = 6
    w_heads = _np.transpose(_np.asarray(L0_gnn_W), (1, 0, 2)).reshape(d, groups, -1)
    w_gate = _np.asarray(L0_gnn_H_w).T.reshape(d, groups, -1)
    laid = {
        "x": x, "adj": adj, "w_all": _np.concatenate([w_heads, w_gate], axis=2),
        "w_src": _np.asarray(L0_gnn_w_src).reshape(heads, e), "w_dst": _np.asarray(L0_gnn_w_dst).reshape(heads, e),
        "b": L0_gnn_b, "h_bias": L0_gnn_H_b,
    }
    nc = _bacc.Bacc("TRN2", target_bir_lowering=False, num_devices=1)
    arrays, args = {}, []
    for name in _INS:
        a = _np.ascontiguousarray(laid[name])
        arrays[f"in_{name}_dram"] = a
        args.append(nc.dram_tensor(f"in_{name}_dram", a.shape, _mybir.dt.from_np(a.dtype), kind="ExternalInput").ap())
    args.append(nc.dram_tensor("out_0_dram", x.shape, _mybir.dt.float32, kind="ExternalOutput").ap())
    gnn_kernel(nc, *args)
    r = _run(nc, [arrays], core_ids=[0])
    return r.results[0]["out_0_dram"]
```
